# Optimizing a Trainium2 kernel written in Bass

```python
import numpy as np
import jax
import jax.numpy as jnp

def _softmax(x, axis=-1):
    return jax.nn.softmax(x, axis=axis)

def _gelu(x):
    return jax.nn.gelu(x, approximate=True)

def _silu(x):
    return jax.nn.silu(x)

def _sigmoid(x):
    return jax.nn.sigmoid(x)

def _layernorm(x, axis=-1, eps=1e-05):
    m = jnp.mean(x, axis=axis, keepdims=True)
    v = jnp.var(x, axis=axis, keepdims=True)
    return (x - m) / jnp.sqrt(v + eps)

def _scatter_add(tgt, idx, src, axis=0):
    return tgt.at[idx].add(src)

def _segment_sum(src, seg, n):
    return jax.ops.segment_sum(src, seg, n)
kernel_name = 'mk_early_fusion_d1_tok_img512_r4_53794f'

def setup_inputs(seed: int=0):
    np.random.seed(seed)
    _w = jnp.asarray

    def _rec_inputs():
        import jax
        import jax.numpy as jnp
        _rk = jax.random.key(seed)
        x = -0.000222058 + 0.999998 * jax.random.normal(jax.random.fold_in(_rk, 1), (16, 3, 64, 64), jnp.float32)
        txt = -0.000382491 + 0.999131 * jax.random.normal(jax.random.fold_in(_rk, 2), (16, 128, 128), jnp.float32)
        return (x, txt)
    x, txt = _rec_inputs()

    def _L0_tok_setup():
        import jax, jax.numpy as jnp
        import numpy as np
        IMG, P, C, D = (64, 16, 3, 128)
        NP = (IMG // P) ** 2
        PD = P * P * C
        key = jax.random.key(seed)
        k1, k2, k3 = jax.random.split(key, 3)
        x = jax.random.normal(k1, (128, C, IMG, IMG), dtype=jnp.float32)
        W = jax.random.normal(k2, (D, PD), dtype=jnp.float32) * (1.0 / np.sqrt(PD))
        b = jax.random.normal(k3, (D,), dtype=jnp.float32) * 0.01
        return {'x': x, 'W': W, 'b': b}
    _L0_tok_all = _L0_tok_setup()
    _L0_tok_in = {k: v for k, v in _L0_tok_all.items() if k in ('W', 'b')}
    del _L0_tok_all

    def _L0_attn_setup():
        import jax, jax.numpy as jnp
        import numpy as np
        DIM = 128
        HEADS = 8
        DIM_HEAD = 16
        SCALE = DIM_HEAD ** (-0.5)
        EPS = 1e-05
        SQRT_HALF = 0.5 ** 0.5

        def second_taylor_expansion(t):
            b, h, n, d = t.shape
            x0 = jnp.ones((b, h, n, 1), dtype=t.dtype)
            x2 = (jnp.einsum('bhni,bhnj->bhnij', t, t) * SQRT_HALF).reshape(b, h, n, d * d)
            return jnp.concatenate([x0, t, x2], axis=-1)
        key = jax.random.key(seed)
        k1, k2, k3, k4 = jax.random.split(key, 4)
        x = jax.random.normal(k1, (1, 512, DIM), dtype=jnp.float32)
        w_q = jax.random.normal(k2, (DIM, HEADS * DIM_HEAD), dtype=jnp.float32) * 0.02
        w_kv = jax.random.normal(k3, (DIM, 2 * HEADS * DIM_HEAD), dtype=jnp.float32) * 0.02
        w_out = jax.random.normal(k4, (HEADS * DIM_HEAD, DIM), dtype=jnp.float32) * 0.02
        return {'x': x, 'w_q': w_q, 'w_kv': w_kv, 'w_out': w_out}
    _L0_attn_all = _L0_attn_setup()
    _L0_attn_in = {k: v for k, v in _L0_attn_all.items() if k in ('w_q', 'w_kv', 'w_out')}
    del _L0_attn_all

    def _L0_ffn_setup():
        import jax, jax.numpy as jnp
        import numpy as np
        import math
        D_MODEL = 128
        N_EXPERTS = 128
        TOP_K = 8
        N_HEADS = 8
        D_KEYS = 128
        HALF = D_KEYS // 2
        N_BATCH, T_SEQ = (2, 512)
        key = jax.random.key(seed)
        k1, k2, k3, k4, k5, k6 = jax.random.split(key, 6)
        queries = jax.random.normal(k1, (N_BATCH, T_SEQ, D_MODEL), dtype=jnp.float32)
        bound_q = 1.0 / math.sqrt(D_MODEL)
        Wq = jax.random.uniform(k2, (N_HEADS * D_KEYS, D_MODEL), minval=-bound_q, maxval=bound_q, dtype=jnp.float32)
        bq = jax.random.uniform(k3, (N_HEADS * D_KEYS,), minval=-bound_q, maxval=bound_q, dtype=jnp.float32)
        bound_k = 1.0 / math.sqrt(HALF)
        keys = jax.random.uniform(k4, (N_HEADS, 2, N_EXPERTS, HALF), minval=-bound_k, maxval=bound_k, dtype=jnp.float32)
        std = D_MODEL ** (-0.5)
        w_down_embed = std * jax.random.normal(k5, (N_EXPERTS * N_EXPERTS, D_MODEL), dtype=jnp.float32)
        w_up_embed = std * jax.random.normal(k6, (N_EXPERTS * N_EXPERTS, D_MODEL), dtype=jnp.float32)
        return {'queries': queries, 'Wq': Wq, 'bq': bq, 'keys': keys, 'w_down_embed': w_down_embed, 'w_up_embed': w_up_embed}
    _L0_ffn_all = _L0_ffn_setup()
    _L0_ffn_in = {k: v for k, v in _L0_ffn_all.items() if k in ('Wq', 'bq', 'keys', 'w_down_embed', 'w_up_embed')}
    del _L0_ffn_all
    return {'x': x, 'txt': txt, 'L0_tok_W': _L0_tok_in['W'], 'L0_tok_b': _L0_tok_in['b'], 'L0_attn_w_q': _L0_attn_in['w_q'], 'L0_attn_w_kv': _L0_attn_in['w_kv'], 'L0_attn_w_out': _L0_attn_in['w_out'], 'L0_ffn_Wq': _L0_ffn_in['Wq'], 'L0_ffn_bq': _L0_ffn_in['bq'], 'L0_ffn_keys': _L0_ffn_in['keys'], 'L0_ffn_w_down_embed': _L0_ffn_in['w_down_embed'], 'L0_ffn_w_up_embed': _L0_ffn_in['w_up_embed']}

def reference(x, txt, L0_tok_W, L0_tok_b, L0_attn_w_q, L0_attn_w_kv, L0_attn_w_out, L0_ffn_Wq, L0_ffn_bq, L0_ffn_keys, L0_ffn_w_down_embed, L0_ffn_w_up_embed):
    import jax
    import jax.numpy as jnp

    def _L0_tok_ref(x, W, b):
        import jax, jax.numpy as jnp
        import numpy as np
        IMG, P, C, D = (64, 16, 3, 128)
        NP = (IMG // P) ** 2
        PD = P * P * C
        B, c, H, Wd = x.shape
        xp = x.reshape(B, c, H // P, P, Wd // P, P)
        xp = xp.transpose(0, 2, 4, 1, 3, 5).reshape(B, NP, c * P * P)
        return jnp.einsum('bnk,dk->bnd', xp, W) + b

    def _L0_attn_ref(x, w_q, w_kv, w_out):
        import jax, jax.numpy as jnp
        import numpy as np
        DIM = 128
        HEADS = 8
        DIM_HEAD = 16
        SCALE = DIM_HEAD ** (-0.5)
        EPS = 1e-05
        SQRT_HALF = 0.5 ** 0.5

        def second_taylor_expansion(t):
            b, h, n, d = t.shape
            x0 = jnp.ones((b, h, n, 1), dtype=t.dtype)
            x2 = (jnp.einsum('bhni,bhnj->bhnij', t, t) * SQRT_HALF).reshape(b, h, n, d * d)
            return jnp.concatenate([x0, t, x2], axis=-1)
        b, n, _ = x.shape
        q = (x @ w_q).reshape(b, n, HEADS, DIM_HEAD).transpose(0, 2, 1, 3)
        kv = (x @ w_kv).reshape(b, n, 2, HEADS, DIM_HEAD)
        k = kv[:, :, 0].transpose(0, 2, 1, 3)
        v = kv[:, :, 1].transpose(0, 2, 1, 3)
        q = q * SCALE
        qf = second_taylor_expansion(q)
        kf = second_taylor_expansion(k)
        kv_outer = jnp.einsum('bhnd,bhne->bhnde', kf, v)
        kv_cum = jnp.cumsum(kv_outer, axis=2)
        num = jnp.einsum('bhnd,bhnde->bhne', qf, kv_cum)
        k_cum = jnp.cumsum(kf, axis=2)
        den = jnp.einsum('bhnd,bhnd->bhn', qf, k_cum)
        out = num / jnp.maximum(den, EPS)[..., None]
        out = out.transpose(0, 2, 1, 3).reshape(b, n, HEADS * DIM_HEAD)
        return out @ w_out

    def _L0_ffn_ref(queries, Wq, bq, keys, w_down_embed, w_up_embed):
        import jax, jax.numpy as jnp
        import numpy as np
        import math
        D_MODEL = 128
        N_EXPERTS = 128
        TOP_K = 8
        N_HEADS = 8
        D_KEYS = 128
        HALF = D_KEYS // 2
        N_BATCH, T_SEQ = (2, 512)
        N, T, D = queries.shape
        H, E, K = (N_HEADS, N_EXPERTS, TOP_K)
        q_tok = queries.reshape(-1, D)
        qh = q_tok @ Wq.T + bq
        qh = qh.reshape(-1, H, 2, HALF)
        sub_scores = jnp.einsum('nhcf,hcef->nhce', qh, keys)
        s, idx = jax.lax.top_k(sub_scores, K)
        all_scores = (s[:, :, 0, :, None] + s[:, :, 1, None, :]).reshape(-1, H, K * K)
        all_idx = (idx[:, :, 0, :, None] * E + idx[:, :, 1, None, :]).reshape(-1, H, K * K)
        best_s, best_pos = jax.lax.top_k(all_scores, K)
        indices = jnp.take_along_axis(all_idx, best_pos, axis=-1)
        w_down = w_down_embed[indices]
        w_up = w_up_embed[indices]
        x = jnp.einsum('nd,nhkd->nhk', q_tok, w_down)
        x = jax.nn.gelu(x)
        vals = x * jax.nn.softmax(best_s, axis=-1)
        out = jnp.einsum('nhk,nhkd->nd', vals, w_up)
        return out.reshape(N, T, D)
    h = _L0_tok_ref(x, L0_tok_W, L0_tok_b)
    h = jnp.concatenate([h, txt], axis=1)
    h = h + _L0_attn_ref(_layernorm(h, axis=-1), L0_attn_w_q, L0_attn_w_kv, L0_attn_w_out)
    h = h + _L0_ffn_ref(_layernorm(h, axis=-1), L0_ffn_Wq, L0_ffn_bq, L0_ffn_keys, L0_ffn_w_down_embed, L0_ffn_w_up_embed)
    return h

_drawn_inputs = setup_inputs


def setup_inputs(seed=0):
    import zlib

    import numpy as np

    out = dict(_drawn_inputs(seed))
    spreads = {}
    factors = {'L0_tok_b': 8.0, 'L0_attn_w_q': 8.0, 'L0_attn_w_kv': 4.389, 'L0_attn_w_out': 4.5}
    for name, (base, spread) in spreads.items():
        noise = np.random.default_rng([zlib.crc32(name.encode()), seed]).standard_normal(out[name].shape)
        drawn = base * np.exp(spread * noise) if base else spread * noise
        out[name] = jnp.asarray(drawn.astype(out[name].dtype))
    for name, factor in factors.items():
        out[name] = (out[name] * factor).astype(out[name].dtype)
    return out
```

```python
from contextlib import ExitStack

import concourse.bass as bass
from concourse import mybir
from concourse.alu_op_type import AluOpType as ALU

F32 = mybir.dt.float32
U32 = mybir.dt.uint32
I32 = mybir.dt.int32
ACT = mybir.ActivationFunctionType
AX_X = mybir.AxisListType.X

P = 128
D = 128
BATCH, PATCHES, TEXT = 16, 16, 128
PD = 768
PC = PD // P
H, DH = 8, 16
HL, HG = 4, 2
PH, HALF, E, K = 8, 64, 128, 8
NK = PH * K
PATCH_TILES = BATCH * PATCHES // P
TILES = PATCH_TILES + BATCH
EPS = 1e-5
QSCALE = DH ** -0.5
PAIRS = [(a, b) for a in range(K) for b in range(K) if (a + 1) * (b + 1) <= K]
NC = len(PAIRS)
GELU_A, GELU_B = 0.7978845608028654, 0.044715
HALVES = 2
CH = NK // HALVES
RSQRT_SEED = 1597463007.0
NEWTON = 3


def program(nc, patches, txt, tok_w, tok_b, w_q, w_kv, w_out, wq_ffn, bq, keys, table, out):
    ctx = ExitStack()
    with ctx:
        def sb(name, shape, dt=F32):
            return ctx.enter_context(nc.sbuf_tensor(name, shape, dt))

        def ps(name, shape):
            return ctx.enter_context(nc.psum_tensor(name, shape, F32))

        def sem(name):
            return ctx.enter_context(nc.semaphore(name))

        wtok = sb("wtok", [P, PC, D])
        xpat = sb("xpat", [P, PC, BATCH * PATCHES])
        btok = sb("btok", [1, D])
        ones = sb("ones", [1, P])
        wqk_in = sb("wqk_in", [P, 3 * D])
        wqk = sb("wqk", [P, 2, HG, HL, 32])
        wout = sb("wout", [P, D])
        wqf = sb("wqf", [P, PH, D])
        bqf = sb("bqf", [P, PH])
        keysT = sb("keysT", [P, PH, E])
        mt = sb("mt", [P, 2, PH * E])
        brow = sb("brow", [1, 2, PH * E])
        ident = sb("ident", [P, P])
        tri = sb("tri", [P, P])
        blk = sb("blk", [P, P])
        cand_no = sb("cand_no", [P, NC])
        h0 = sb("h0", [P, 2, D])
        h1 = sb("h1", [P, 2, D])
        stats = sb("stats", [P, 6])
        mv = sb("mv", [P, 2])
        hv = sb("hv", [P, 1])
        bits = sb("bits", [P, 1], I32)
        y = sb("y", [P, 1])
        yt = sb("yt", [P, 1])
        xn = sb("xn", [P, D])
        xnT = sb("xnT", [P, P])
        qkT = sb("qkT", [P, 2 * HG, P])
        keep = sb("keep", [P, BATCH, 3, PATCHES])
        cur = sb("cur", [P, 3, PATCHES])
        va = sb("va", [P, H, DH + 1])
        vpa = sb("vpa", [PATCHES, H, DH + 1])
        pT = sb("pT", [P, H, P])
        pTp = sb("pTp", [PATCHES, H, P])
        rden = sb("rden", [P, H])
        on = sb("on", [P, H, DH])
        onT = sb("onT", [P, P])
        q2 = sb("q2", [P, D])
        q2T = sb("q2T", [P, P])
        top = sb("top", [P, 2, 2, PH, K])
        top_i = sb("top_i", [P, 2, PH, K], U32)
        cand = sb("cand", [P, 2, PH, NC])
        best = sb("best", [P, PH, K])
        best_p = sb("best_p", [P, PH, K], U32)
        best_f = sb("best_f", [P, NK])
        hit = sb("hit", [P, NK, NC])
        idx = sb("idx", [P, 2, NK], U32)
        dif = sb("dif", [P, PH, K])
        ex = sb("ex", [P, PH, K])
        sm = sb("sm", [P, PH])
        wts = sb("wts", [P, 2, NK])
        rows = sb("rows", [P, 2, NK, 2 * D])
        prod = sb("prod", [P, K, D])
        x = sb("x", [P, NK])
        u = sb("u", [P, NK])
        th = sb("th", [P, NK])
        vals = sb("vals", [P, NK])
        res = sb("res", [P, 2, D])
        red = sb("red", [P, D])

        A = ps("A", [P, 4, 512])
        B = ps("B", [P, 512])
        C = ps("C", [P, 512])
        Q = ps("Q", [P, 2, D])
        ACC = ps("ACC", [P, 4, D])

        s_tok, s_attn_w, s_ffn_w = sem("s_tok"), sem("s_attn_w"), sem("s_ffn_w")
        s_txt = [sem("s_txt0"), sem("s_txt1")]
        s_pool, s_const, s_wqk, s_fold, s_fold_c = sem("s_pool"), sem("s_const"), sem("s_wqk"), sem("s_fold"), sem("s_fold_c")
        s_dveset = sem("s_dveset")
        s_emb, s_xn, s_xnT_p, s_xnT = sem("s_emb"), sem("s_xn"), sem("s_xnT_p"), sem("s_xnT")
        s_qk_p, s_qk, s_v_p, s_v = sem("s_qk_p"), sem("s_qk"), sem("s_v_p"), sem("s_v")
        s_cur, s_s_p, s_sq, s_p = sem("s_cur"), sem("s_s_p"), sem("s_sq"), sem("s_p")
        s_o_p, s_on, s_onT_p, s_onT, s_y_p = sem("s_o_p"), sem("s_on"), sem("s_onT_p"), sem("s_onT"), sem("s_y_p")
        s_h1, s_q2, s_q2T_p, s_q2T, s_sc_p = sem("s_h1"), sem("s_q2"), sem("s_q2T_p"), sem("s_q2T"), sem("s_sc_p")
        s_topk, s_idx, s_dif, s_ex = sem("s_topk"), sem("s_idx"), sem("s_dif"), sem("s_ex")
        s_rows = [[sem(f"s_rows{p}_{c}") for c in range(PH)] for p in range(2)]
        s_u, s_th, s_vals, s_scaled, s_acc = sem("s_u"), sem("s_th"), sem("s_vals"), sem("s_scaled"), sem("s_acc")
        s_res, s_used = sem("s_res"), sem("s_used")
        s_out = [sem("s_out0"), sem("s_out1")]
        s_gathering, s_searching = sem("s_gathering"), sem("s_searching")
        s_dve = sem("s_dve")

        block = ctx.enter_context(nc.Block())
        LAST_PAIR = (TILES - PATCH_TILES) // 2

        @block.sync
        def _(sp):
            def load_txt(b, par):
                sp.dma_start(h0[:, par, :], txt[b, :, :]).then_inc(s_txt[par], 16)

            def store_patch(g):
                for j in range(P // PATCHES):
                    sp.dma_start(out[g * (P // PATCHES) + j, 0:PATCHES, :],
                                 res[j * PATCHES:(j + 1) * PATCHES, g, :]).then_inc(s_out[g], 16)

            def store_txt(b, par):
                sp.dma_start(out[b, PATCHES:PATCHES + TEXT, :], res[:, par, :]).then_inc(s_out[par], 16)

            sp.dma_start(xpat[:], patches).then_inc(s_tok, 16)
            sp.dma_start(wtok[:], tok_w).then_inc(s_tok, 16)
            sp.dma_start(btok[:], tok_b).then_inc(s_tok, 16)
            sp.dma_start(wqf[:], wq_ffn).then_inc(s_ffn_w, 16)
            sp.dma_start(keysT[:], keys).then_inc(s_ffn_w, 16)
            sp.dma_start(bqf[:], bq).then_inc(s_ffn_w, 16)
            for t in range(3):
                sp.wait_ge(s_h1, t + 1)
                load_txt(t, t % 2)
                if t >= 1:
                    sp.wait_ge(s_res, t)
                    store_patch(t - 1)
            with sp.Fori(0, (BATCH - 4) // 2) as i:
                for s in range(2):
                    t = i * 2 + (3 + s)
                    sp.wait_ge(s_h1, t + 1)
                    load_txt(t, (3 + s) % 2)
                    sp.wait_ge(s_res, t)
                    store_txt(t - 3, (3 + s + 1) % 2)
            for t in range(BATCH - 1, TILES + 1):
                if t < BATCH:
                    sp.wait_ge(s_h1, t + 1)
                    load_txt(t, t % 2)
                sp.wait_ge(s_res, t)
                store_txt(t - 3, (t - 1) % 2)
            for p in range(2):
                sp.wait_ge(s_out[p], 16 * (P // PATCHES + BATCH // 2))

        @block.gpsimd
        def _(pool):
            pool_count = [0]

            def link(ins):
                pool_count[0] += 1
                ins.then_inc(s_pool, 1)
                pool.wait_ge(s_pool, pool_count[0])

            link(nc.gpsimd.memset(ident[:], 0.0))
            link(nc.gpsimd.affine_select(out=ident[:], in_=ident[:], compare_op=ALU.not_equal, fill=1.0, base=0,
                                         pattern=[[-1, P]], channel_multiplier=1))
            link(nc.gpsimd.memset(tri[:], 1.0))
            link(nc.gpsimd.affine_select(out=tri[:], in_=tri[:], compare_op=ALU.is_ge, fill=0.0, base=0,
                                         pattern=[[1, P]], channel_multiplier=-1))
            blocks = blk[:].rearrange("p (b j) -> p b j", j=PATCHES)
            tris = tri[:].rearrange("p (b j) -> p b j", j=PATCHES)
            link(nc.gpsimd.affine_select(out=blocks, in_=tris, compare_op=ALU.is_ge, fill=0.0, base=0,
                                         pattern=[[-PATCHES, P // PATCHES], [0, PATCHES]], channel_multiplier=1))
            link(nc.gpsimd.affine_select(out=blocks, in_=blocks, compare_op=ALU.is_ge, fill=0.0, base=PATCHES - 1,
                                         pattern=[[PATCHES, P // PATCHES], [0, PATCHES]], channel_multiplier=-1))
            nc.gpsimd.iota(cand_no[:], pattern=[[1, NC]], base=0, channel_multiplier=0,
                           allow_small_or_imprecise_dtypes=True).then_inc(s_const, 1)

            def gather(t, par):
                pool.wait_ge(s_idx, t + 1)
                pool.sem_inc(s_gathering, 1)
                for c in range(PH):
                    for k in range(c * K, (c + 1) * K):
                        nc.gpsimd.indirect_dma_start(
                            rows[:, par, k, :], None, table,
                            bass.IndirectOffsetOnAxis(ap=idx[:, par, k:k + 1], axis=0)).then_inc(s_rows[par][c], 16)

            for t in range(PATCH_TILES):
                gather(t, t % 2)
            with pool.Fori(0, LAST_PAIR) as i:
                for s in range(2):
                    t = i * 2 + (PATCH_TILES + s)
                    pool.wait_ge(s_used, t - 1)
                    gather(t, s)

        @block.scalar
        def _(act):
            act.dma_start(wqk_in[:, 0:D], w_q).then_inc(s_attn_w, 16)
            act.dma_start(wqk_in[:, D:3 * D], w_kv).then_inc(s_attn_w, 16)
            act.dma_start(wout[:], w_out).then_inc(s_attn_w, 16)

            act.wait_ge(s_fold, 1)
            nc.scalar.copy(mt[:].rearrange("p c n -> p (c n)"), A[:].rearrange("p a n -> p (a n)")).then_inc(s_fold_c, 1)
            act.wait_ge(s_fold, 2)
            nc.scalar.copy(brow[:].rearrange("p c n -> p (c n)"),
                           A[0:1, :, :].rearrange("p a n -> p (a n)")).then_inc(s_fold_c, 1)

            def front(t, patch, b=None):
                act.wait_ge(s_xnT_p, t + 1)
                nc.scalar.copy(xnT[:], C[:, 0:P]).then_inc(s_xnT, 1)
                if patch is None:
                    nc.scalar.copy(cur[:].rearrange("p a j -> p (a j)"),
                                   keep[:, bass.ds(b, 1), :, :].rearrange("p o a j -> p (o a j)")).then_inc(s_cur, 1)
                act.wait_ge(s_qk_p, t + 1)
                nc.scalar.copy(qkT[:].rearrange("p g n -> p (g n)"), B[:]).then_inc(s_qk, 1)
                if patch is not None:
                    act.wait_ge(s_qk, t + 1)
                    act.wait_ge(s_xnT, t + 1)
                    mine = keep[:, patch * 8:(patch + 1) * 8, :, :]
                    for g in range(HG):
                        nc.scalar.copy(mine[:, :, g, :], qkT[:, HG + g, :].rearrange("p (b j) -> p b j", j=PATCHES))
                    nc.scalar.copy(mine[:, :, 2, :],
                                   xnT[:].rearrange("p (b j) -> p b j", j=PATCHES)).then_inc(s_cur, 1)
                act.wait_ge(s_s_p, t + 1)
                last = nc.scalar.activation(pT[:].rearrange("p (l g) n -> p l (g n)", g=HG), A[:, :, 0:HG * P],
                                            ACT.Square, bias=1.0, scale=QSCALE)
                if patch is None:
                    last = nc.scalar.activation(pTp[:].rearrange("p (l g) n -> p l (g n)", g=HG),
                                                A[0:PATCHES, :, HG * P:2 * HG * P], ACT.Square, bias=1.0, scale=QSCALE)
                last.then_inc(s_sq, 1)
                act.wait_ge(s_onT_p, t + 1)
                nc.scalar.copy(onT[:], C[:, 0:P]).then_inc(s_onT, 1)
                act.wait_ge(s_q2T_p, t + 1)
                nc.scalar.copy(q2T[:], C[:, 2 * P:3 * P]).then_inc(s_q2T, 1)
                act.wait_ge(s_dif, t + 1)
                nc.scalar.activation(ex[:], dif[:], ACT.Exp).then_inc(s_ex, 1)

            def back(t, par):
                for n in range(HALVES):
                    act.wait_ge(s_u, t * HALVES + (n + 1))
                    nc.scalar.activation(th[:, n * CH:(n + 1) * CH], u[:, n * CH:(n + 1) * CH], ACT.Tanh,
                                         scale=GELU_A).then_inc(s_th, 1)
                    act.wait_ge(s_vals, t * HALVES + (n + 1))
                    for k in range(n * CH, (n + 1) * CH):
                        up = rows[:, par, k, D:2 * D]
                        last = nc.scalar.activation(up, up, ACT.Copy, scale=vals[:, k:k + 1])
                        if k % 4 == 3:
                            last.then_inc(s_scaled, 1)

            front(0, 0)
            front(1, 1)
            back(0, 0)
            with act.Fori(0, LAST_PAIR) as i:
                for s in range(2):
                    t = i * 2 + (PATCH_TILES + s)
                    front(t, None, t - PATCH_TILES)
                    back(t - 1, (s + 1) % 2)
            back(TILES - 1, (TILES - 1) % 2)

        @block.vector
        def _(dve):
            count = [0]

            def link(ins):
                count[0] += 1
                ins.then_inc(s_dve, 1)
                dve.wait_ge(s_dve, count[0])

            def clear():
                dve.sem_clear(s_dve)
                count[0] = 0

            def layernorm(dst, src, done):
                link(nc.vector.bn_stats(stats[:], src))
                link(nc.vector.bn_aggr(mv[:], stats[:]))
                link(nc.vector.tensor_scalar(yt[:], mv[:, 1:2], EPS, None, ALU.add))
                link(nc.vector.tensor_scalar(bits[:], yt[:].bitcast(I32), 1, None, ALU.logical_shift_right))
                nc.vector.tensor_scalar(y[:].bitcast(I32), bits[:], -1.0, RSQRT_SEED, ALU.mult, ALU.add)
                link(nc.vector.tensor_scalar(hv[:], yt[:], -0.5, None, ALU.mult))
                for _ in range(NEWTON):
                    link(nc.vector.scalar_tensor_tensor(yt[:], y[:], hv[:], y[:], ALU.mult, ALU.mult))
                    link(nc.vector.scalar_tensor_tensor(y[:], yt[:], 1.5, y[:], ALU.add, ALU.mult))
                nc.vector.tensor_scalar(dst, src, mv[:, 0:1], y[:], ALU.subtract, ALU.mult).then_inc(done, 1)

            dve.wait_ge(s_const, 1)
            nc.vector.memset(ones[:], 1.0)
            nc.vector.memset(va[:], 1.0)
            nc.vector.memset(vpa[:], 1.0)
            link(nc.vector.memset(wqk[:], 0.0))
            dve.wait_ge(s_attn_w, 48)
            nc.vector.tensor_copy(wqk[:].rearrange("p a g l j -> p (a g l) j")[:, :, 0:DH],
                                  wqk_in[:, 0:2 * D].rearrange("p (a j) -> p a j", j=DH)).then_inc(s_wqk, 1)
            clear()

            def front(t, patch, par):
                src = h0[:, par, :]
                if patch is not None:
                    dve.wait_ge(s_emb, t + 1)
                    link(nc.vector.tensor_copy(src, C[:, 3 * P:4 * P]))
                else:
                    dve.wait_ge(s_txt[par], (t - par) * 8)
                layernorm(xn[:], src, s_xn)
                dve.wait_ge(s_v_p, t + 1)
                last = nc.vector.tensor_copy(va[:, :, 0:DH], C[:, P:2 * P].rearrange("p (h j) -> p h j", j=DH))
                if patch is None:
                    last = nc.vector.tensor_copy(vpa[:, :, 0:DH],
                                                 C[0:PATCHES, 2 * P:3 * P].rearrange("p (h j) -> p h j", j=DH))
                last.then_inc(s_v, 1)
                dve.wait_ge(s_sq, t + 1)
                mask = (tri if patch is None else blk)[:].unsqueeze(1).to_broadcast([P, H, P])
                last = nc.vector.scalar_tensor_tensor(pT[:], pT[:], 1.0, mask, ALU.add, ALU.mult)
                if patch is None:
                    last = nc.vector.tensor_scalar(pTp[:], pTp[:], 1.0, None, ALU.add)
                last.then_inc(s_p, 1)
                dve.wait_ge(s_o_p, t + 1)
                o = B[:, 0:H * (DH + 1)].rearrange("p (h j) -> p h j", j=DH + 1)
                link(nc.vector.tensor_scalar(rden[:].unsqueeze(2), o[:, :, DH:DH + 1], 2 * EPS, None, ALU.max))
                link(nc.vector.reciprocal(rden[:], rden[:]))
                nc.vector.tensor_tensor(on[:], o[:, :, 0:DH], rden[:].unsqueeze(2).to_broadcast([P, H, DH]),
                                        ALU.mult).then_inc(s_on, 1)
                dve.wait_ge(s_y_p, t + 1)
                nc.vector.tensor_tensor(h1[:, par, :], h0[:, par, :], C[:, P:2 * P], ALU.add).then_inc(s_h1, 1)
                dve.wait_ge(s_h1, t + 1)
                layernorm(q2[:], h1[:, par, :], s_q2)
                dve.wait_ge(s_q2, t + 1)
                nc.vector.tensor_copy(Q[:, par, :], q2[:])
                for a in range(4):
                    dve.wait_ge(s_sc_p, t * 4 + (a + 1))
                    dve.sem_inc(s_searching, 1)
                    for n in range(4 * a, 4 * a + 4):
                        last = nc.vector.max(top[:, 0, n // PH, n % PH, :], A[:, a, (n % 4) * E:(n % 4 + 1) * E])
                link(last)
                for n in range(2 * PH):
                    last = nc.vector.max_index(top_i[:, n // PH, n % PH, :], top[:, 0, n // PH, n % PH, :],
                                               A[:, n // 4, (n % 4) * E:(n % 4 + 1) * E])
                last.then_inc(s_topk, 1)
                dve.wait_ge(s_topk, t + 1)
                nc.vector.tensor_scalar(top[:, 1, 0, :, :], top_i[:, 0, :, :], float(E), None, ALU.mult)
                link(nc.vector.tensor_copy(top[:, 1, 1, :, :], top_i[:, 1, :, :]))
                at = 0
                for a, nb in [(a, K // (a + 1)) for a in range(4)]:
                    last = nc.vector.tensor_tensor(
                        cand[:, :, :, at:at + nb],
                        top[:, :, 0, :, a:a + 1].to_broadcast([P, 2, PH, nb]), top[:, :, 1, :, 0:nb], ALU.add)
                    at += nb
                link(nc.vector.tensor_tensor(cand[:, :, :, at:NC], top[:, :, 0, :, 4:K],
                                             top[:, :, 1, :, 0:1].to_broadcast([P, 2, PH, K - 4]), ALU.add))
                for h in range(PH):
                    last = nc.vector.max(best[:, h, :], cand[:, 0, h, :])
                link(last)
                for h in range(PH):
                    last = nc.vector.max_index(best_p[:, h, :], best[:, h, :], cand[:, 0, h, :])
                link(last)
                link(nc.vector.tensor_copy(best_f[:], best_p[:].rearrange("p h k -> p (h k)")))
                link(nc.vector.tensor_tensor(hit[:], best_f[:].unsqueeze(2).to_broadcast([P, NK, NC]),
                                             cand_no[:].unsqueeze(1).to_broadcast([P, NK, NC]), ALU.is_equal))
                hits = hit[:].rearrange("p (h k) n -> p h k n", k=K)
                link(nc.vector.tensor_tensor(hits, hits, cand[:, 1, :, :].unsqueeze(2).to_broadcast([P, PH, K, NC]),
                                             ALU.mult))
                link(nc.vector.tensor_reduce(best_f[:], hit[:], AX_X, ALU.add))
                nc.vector.tensor_copy(idx[:, par, :], best_f[:]).then_inc(s_idx, 1)
                nc.vector.tensor_tensor(dif[:], best[:], best[:, :, 0:1].to_broadcast([P, PH, K]),
                                        ALU.subtract).then_inc(s_dif, 1)
                dve.wait_ge(s_ex, t + 1)
                link(nc.vector.tensor_reduce(sm[:], ex[:], AX_X, ALU.add))
                link(nc.vector.reciprocal(sm[:], sm[:]))
                link(nc.vector.scalar_tensor_tensor(
                    wts[:, par, :].rearrange("p (h k) -> p h k", k=K), ex[:], 0.5,
                    sm[:].unsqueeze(2).to_broadcast([P, PH, K]), ALU.mult, ALU.mult))
                clear()

            def back(t, par, first=False):
                for n in range(HALVES):
                    for c in range(n * PH // HALVES, (n + 1) * PH // HALVES):
                        dve.wait_ge(s_rows[par][c], (t - par) * (8 * K) + 16 * K)
                        link(nc.vector.tensor_tensor(prod[:], rows[:, par, c * K:(c + 1) * K, 0:D],
                                                     Q[:, par, :].unsqueeze(1).to_broadcast([P, K, D]), ALU.mult))
                        link(nc.vector.tensor_reduce(x[:, c * K:(c + 1) * K], prod[:], AX_X, ALU.add))
                    half = slice(n * CH, (n + 1) * CH)
                    xh, uh, vh = x[:, half], u[:, half], vals[:, half]
                    link(nc.vector.tensor_tensor(uh, xh, xh, ALU.mult))
                    link(nc.vector.tensor_scalar(uh, uh, GELU_B, 1.0, ALU.mult, ALU.add))
                    nc.vector.tensor_tensor(uh, uh, xh, ALU.mult).then_inc(s_u, 1)
                    link(nc.vector.tensor_tensor(xh, xh, wts[:, par, half], ALU.mult))
                    dve.wait_ge(s_th, t * HALVES + (n + 1))
                    nc.vector.scalar_tensor_tensor(vh, th[:, half], 1.0, xh, ALU.add, ALU.mult).then_inc(s_vals, 1)
                dve.wait_ge(s_acc, t + 1)
                link(nc.vector.tensor_reduce(red[:], ACC[:].rearrange("p a d -> p d a"), AX_X, ALU.add))
                if not first:
                    dve.wait_ge(s_out[par], (t - par) * 8 + (P // PATCHES - 1) * 16)
                nc.vector.tensor_tensor(res[:, par, :], red[:], h1[:, par, :], ALU.add).then_inc(s_res, 1)
                dve.wait_ge(s_res, t + 1)
                dve.sem_inc(s_used, 1)
                clear()

            front(0, 0, 0)
            front(1, 1, 1)
            back(0, 0, first=True)
            front(2, None, 0)
            back(1, 1, first=True)
            front(3, None, 1)
            back(2, 0)
            with dve.Fori(0, LAST_PAIR - 1) as i:
                for s in range(2):
                    t = i * 2 + (PATCH_TILES + 2 + s)
                    front(t, None, s)
                    back(t - 1, (s + 1) % 2)
            back(TILES - 1, (TILES - 1) % 2)

        @block.tensor
        def _(pe):
            mm = nc.tensor.matmul

            def head(h):
                return h % HL, h // HL

            pe.wait_ge(s_ffn_w, 48)
            for c in range(2):
                r = slice(c * HALF, (c + 1) * HALF)
                for h in range(PH):
                    last = mm(A[:, 2 * c + h // 4, (h % 4) * E:(h % 4 + 1) * E], wqf[r, h, :], keysT[r, h, :],
                              start=True, stop=True)
            last.then_inc(s_fold, 1)
            pe.wait_ge(s_fold_c, 1)
            for c in range(2):
                r = slice(c * HALF, (c + 1) * HALF)
                for h in range(PH):
                    last = mm(A[0:1, 2 * c + h // 4, (h % 4) * E:(h % 4 + 1) * E], bqf[r, h:h + 1], keysT[r, h, :],
                              start=True, stop=True)
            last.then_inc(s_fold, 1)
            pe.wait_ge(s_fold_c, 2)
            pe.wait_ge(s_wqk, 1)
            pe.wait_ge(s_const, 1)
            pe.wait_ge(s_tok, 48)

            def front(t, patch):
                if patch is not None:
                    for c in range(PC):
                        mm(C[:, 3 * P:4 * P], xpat[:, c, patch * P:(patch + 1) * P], wtok[:, c, :], start=c == 0, stop=False)
                    mm(C[:, 3 * P:4 * P], ones[:], btok[:], start=False, stop=True).then_inc(s_emb, 1)
                pe.wait_ge(s_xn, t + 1)
                nc.tensor.transpose(C[:, 0:P], xn[:], ident[:]).then_inc(s_xnT_p, 1)
                pe.wait_ge(s_xnT, t + 1)
                for n in range(2 * HG):
                    last = mm(B[:, n * P:(n + 1) * P], wqk[:, n // HG, n % HG, :, :].rearrange("p l j -> p (l j)"), xnT[:],
                              start=True, stop=True)
                last.then_inc(s_qk_p, 1)
                last = mm(C[:, P:2 * P], xnT[:], wqk_in[:, 2 * D:3 * D], start=True, stop=True)
                if patch is None:
                    pe.wait_ge(s_cur, t + 1)
                    last = mm(C[0:PATCHES, 2 * P:3 * P], cur[:, 2, :], wqk_in[:, 2 * D:3 * D], start=True, stop=True)
                last.then_inc(s_v_p, 1)
                pe.wait_ge(s_qk, t + 1)
                if not (isinstance(t, int) and t == 0):
                    pe.wait_ge(s_topk, t)
                for h in range(H):
                    l, g = head(h)
                    r = slice(32 * l, 32 * l + DH)
                    last = mm(A[:, l, g * P:(g + 1) * P], qkT[r, HG + g, :], qkT[r, g, :], start=True, stop=True)
                    if patch is None:
                        last = mm(A[0:PATCHES, l, (HG + g) * P:(HG + g + 1) * P], cur[r, g, :], qkT[r, g, :],
                                  start=True, stop=True)
                last.then_inc(s_s_p, 1)
                pe.wait_ge(s_v, t + 1)
                pe.wait_ge(s_p, t + 1)
                for h in range(H):
                    l, g = head(h)
                    to = B[:, h * (DH + 1):(h + 1) * (DH + 1)]
                    last = mm(to, pT[:, l * HG + g, :], va[:, h, :], start=True, stop=patch is not None)
                    if patch is None:
                        last = mm(to, pTp[:, l * HG + g, :], vpa[:, h, :], start=False, stop=True)
                last.then_inc(s_o_p, 1)
                pe.wait_ge(s_on, t + 1)
                nc.tensor.transpose(C[:, 0:P], on[:].rearrange("p h j -> p (h j)"), ident[:]).then_inc(s_onT_p, 1)
                pe.wait_ge(s_onT, t + 1)
                mm(C[:, P:2 * P], onT[:], wout[:], start=True, stop=True).then_inc(s_y_p, 1)
                pe.wait_ge(s_q2, t + 1)
                nc.tensor.transpose(C[:, 2 * P:3 * P], q2[:], ident[:]).then_inc(s_q2T_p, 1)
                pe.wait_ge(s_q2T, t + 1)
                for a in range(4):
                    part = slice((a % 2) * 512, (a % 2 + 1) * 512)
                    mm(A[:, a, :], q2T[:], mt[:, a // 2, part], start=True, stop=False)
                    mm(A[:, a, :], ones[:], brow[:, a // 2, part], start=False, stop=True).then_inc(s_sc_p, 1)

            def back(t, par):
                if not (isinstance(t, int) and t == 0):
                    pe.wait_ge(s_res, t)
                for n in range(NK // 4):
                    pe.wait_ge(s_scaled, t * (NK // 4) + (n + 1))
                    last = mm(ACC[:], ident[:], rows[:, par, 4 * n:4 * n + 4, D:2 * D], start=n == 0,
                              stop=n == NK // 4 - 1)
                last.then_inc(s_acc, 1)

            front(0, 0)
            front(1, 1)
            back(0, 0)
            with pe.Fori(0, LAST_PAIR) as i:
                for s in range(2):
                    t = i * 2 + (PATCH_TILES + s)
                    front(t, None)
                    back(t - 1, (s + 1) % 2)
            back(TILES - 1, (TILES - 1) % 2)


def kernel(x, txt, L0_tok_W, L0_tok_b, L0_attn_w_q, L0_attn_w_kv, L0_attn_w_out, L0_ffn_Wq, L0_ffn_bq,
           L0_ffn_keys, L0_ffn_w_down_embed, L0_ffn_w_up_embed):
    import numpy as np
    import concourse.bacc as bacc
    from concourse.bass_utils import run_bass_kernel_spmd

    con = np.ascontiguousarray
    side = 4
    pat = np.asarray(x).reshape(BATCH, 3, side, 16, side, 16).transpose(1, 3, 5, 0, 2, 4)
    pat = con(pat.reshape(PC, P, BATCH * PATCHES).transpose(1, 0, 2))
    arrays = {
        "patches": pat,
        "txt": con(txt),
        "tok_w": con(np.asarray(L0_tok_W).T.reshape(PC, P, D).transpose(1, 0, 2)),
        "tok_b": con(np.asarray(L0_tok_b).reshape(1, D)),
        "w_q": con(L0_attn_w_q),
        "w_kv": con(L0_attn_w_kv),
        "w_out": con(L0_attn_w_out),
        "wq_ffn": con(np.asarray(L0_ffn_Wq).reshape(PH, P, D).transpose(1, 0, 2)),
        "bq": con(np.asarray(L0_ffn_bq).reshape(PH, P).T),
        "keys": con(np.asarray(L0_ffn_keys).transpose(1, 3, 0, 2).reshape(P, PH, E)),
        "table": con(np.concatenate([L0_ffn_w_down_embed, L0_ffn_w_up_embed], axis=1)),
    }
    nc = bacc.Bacc("TRN2", target_bir_lowering=False, num_devices=1)
    aps = [nc.dram_tensor(f"in_{n}", a.shape, F32, kind="ExternalInput").ap() for n, a in arrays.items()]
    o = nc.dram_tensor("out_0", (BATCH, PATCHES + TEXT, D), F32, kind="ExternalOutput").ap()
    program(nc, *aps, o)
    r = run_bass_kernel_spmd(nc, [{f"in_{n}": a for n, a in arrays.items()}], core_ids=[0])
    return r.results[0]["out_0"]
```

```python
from contextlib import ExitStack

import concourse.bass as bass
from concourse import mybir
from concourse.alu_op_type import AluOpType as ALU

F32 = mybir.dt.float32
BF16 = mybir.dt.bfloat16
U32 = mybir.dt.uint32
I32 = mybir.dt.int32
ACT = mybir.ActivationFunctionType
AX_X = mybir.AxisListType.X

P = 128
D = 128
BATCH, PATCHES, TEXT = 16, 16, 128
PD = 768
PC = PD // P
H, DH = 8, 16
HL, HG = 4, 2
PH, HALF, E, K = 8, 64, 128, 8
NK = PH * K
PATCH_TILES = BATCH * PATCHES // P
TILES = PATCH_TILES + BATCH
GROUP = 4
GROUPS = BATCH // GROUP
GATHERED = GROUP - 1
EPS = 1e-5
QSCALE = DH ** -0.5
PAIRS = [(a, b) for a in range(K) for b in range(K) if (a + 1) * (b + 1) <= K]
NC = len(PAIRS)
QUARTERS = 4
CH = NK // QUARTERS
RSQRT_SEED = 1597463007.0
NEWTON = 3
SL = 4
SLICES = E // SL
TP = SL // 2
WBUF = 8
HOTS_BUF = 7
GELU_BUF = 6


def program(nc, patches, txt, tok_w, tok_b, w_q, w_kv, w_out, wq_ffn, bq, keys, table,
            down_t, up_t, out):
    ctx = ExitStack()
    with ctx:
        def sb(name, shape, dt=F32):
            return ctx.enter_context(nc.sbuf_tensor(name, shape, dt))

        def ps(name, shape):
            return ctx.enter_context(nc.psum_tensor(name, shape, F32))

        def sem(name):
            return ctx.enter_context(nc.semaphore(name))

        btok = sb("btok", [1, D])
        ones = sb("ones", [1, P])
        wv = sb("wv", [P, D])
        wqk = sb("wqk", [P, 2, HG, HL, 32])
        wout = sb("wout", [P, D])
        bqf = sb("bqf", [P, PH])
        mt = sb("mt", [P, 2, PH * E])
        bias = sb("bias", [P, 2 * PH])
        bparts = sb("bparts", [P, 3, 2 * PH], BF16)
        own = sb("own", [3 * 2 * PH, 2 * PH])
        brows = sb("brows", [3 * 2 * PH, 2 * PH, E], BF16)
        ones_b = sb("ones_b", [3 * 2 * PH, P], BF16)
        ident_b = sb("ident_b", [P, P], BF16)
        ident = sb("ident", [P, P])
        tri = sb("tri", [P, P])
        blk = sb("blk", [P, P])
        number = sb("number", [P, P])
        h0 = sb("h0", [P, 2, D])
        stats = sb("stats", [P, 6])
        mv = sb("mv", [P, 2])
        hv = sb("hv", [P, 1])
        bits = sb("bits", [P, 1], I32)
        y = sb("y", [P, 1])
        yt = sb("yt", [P, 1])
        xn = sb("xn", [P, D])
        xnT = sb("xnT", [P, P])
        qkT = sb("qkT", [P, 2 * HG, P])
        keep = sb("keep", [P, BATCH, 3, PATCHES])
        cur = sb("cur", [P, 3, PATCHES])
        va = sb("va", [P, H, DH + 1])
        vpa = sb("vpa", [PATCHES, H, DH + 1])
        pT = sb("pT", [P, H, P])
        hit = sb("hit", [P, NK, NC])
        pTp = hit[0:PATCHES, :, :].rearrange("p a b -> p (a b)")[:, 0:H * P].rearrange("p (h n) -> p h n", n=P)
        rden = sb("rden", [P, H])
        on = sb("on", [P, H, DH])
        onT = sb("onT", [P, P])
        q2 = sb("q2", [P, D])
        q2T = sb("q2T", [P, P])
        top = sb("top", [P, 2, 2, PH, K])
        top_i = sb("top_i", [P, 2, PH, K], U32)
        cand = sb("cand", [P, 2, PH, NC])
        best = sb("best", [P, PH, K])
        best_p = sb("best_p", [P, PH, K], U32)
        best_f = sb("best_f", [P, NK])
        dif = sb("dif", [P, PH, K])
        ex = dif
        sm = sb("sm", [P, PH])
        idx = sb("idx", [P, GATHERED, NK], U32)
        wts = sb("wts", [P, GATHERED, NK])
        h1 = sb("h1", [P, GATHERED, D])
        qin = sb("qin", [P, GATHERED, D])
        rows = sb("rows", [P, NK, 2 * D])
        x = sb("x", [P, NK])
        g = sb("g", [P, NK])
        vals = sb("vals", [P, NK])
        res = sb("res", [P, GATHERED, D])
        h1d = sb("h1d", [P, D])
        q2Td = sb("q2Td", [P, P])
        lots = hit[:].rearrange("p a b -> p (a b)")[:, 0:6 * NK].rearrange("p (a h k) -> p a h k", a=3, h=2)
        ij = hit[:].rearrange("p a b -> p (a b)")[:, 6 * NK:8 * NK].bitcast(I32).rearrange("p (a k) -> p a k", a=2)
        wtd = sb("wtd", [P, NK])
        scal = sb("scal", [P, 4, NK])
        stage = sb("stage", [P, HOTS_BUF, 4 * TP * E])
        hot_ij = stage[:, :, 0:2 * TP * E].rearrange("p b (a n e) -> p b a n e", a=2, n=TP)
        hot_w = stage[:, :, 2 * TP * E:4 * TP * E].rearrange("p b (n h e) -> p b n h e", n=TP, h=2)
        halves = stage[:].rearrange("p b (c m) -> p (b c) m", c=2)
        act_x = halves[:, 0:GELU_BUF, :]
        wbuf = halves[:, GELU_BUF:GELU_BUF + WBUF, :]
        gd = sb("gd", [P, E * P])
        gd_j = gd[:].rearrange("p (j n) -> p j n", n=P)
        gd_h = gd[:].rearrange("p (j h n) -> p j h n", h=2, n=P // 2)
        resd = sb("resd", [P, D])
        at = [0]

        def early(*shape):
            n = 1
            for v in shape:
                n *= v
            view = gd[:, at[0]:at[0] + n]
            at[0] += n
            return view.rearrange("p (a b) -> p a b", b=shape[-1])

        wqk_in = early(1, 2 * D)
        wtok, xpat = early(PC, D), early(PC, BATCH * PATCHES)
        wqf, keysT = early(PH, D), early(PH, E)

        A = ps("A", [P, 4, 512])
        B = ps("B", [P, 512])
        ACC = ps("ACC", [P, 4, D])
        X = ps("X", [P, 2, 512])

        s_tok, s_attn_w, s_ffn_w = sem("s_tok"), sem("s_attn_w"), sem("s_ffn_w")
        s_txt = [sem("s_txt0"), sem("s_txt1")]
        s_pool, s_const, s_wqk, s_ones = sem("s_pool"), sem("s_const"), sem("s_wqk"), sem("s_ones")
        s_fold, s_fold_c = sem("s_fold"), sem("s_fold_c")
        s_bias_split, s_bias = sem("s_bias_split"), sem("s_bias")
        s_emb, s_xn, s_xnT_p, s_xnT = sem("s_emb"), sem("s_xn"), sem("s_xnT_p"), sem("s_xnT")
        s_qk_p, s_qk, s_v_p, s_v = sem("s_qk_p"), sem("s_qk"), sem("s_v_p"), sem("s_v")
        s_cur, s_s_p, s_sq, s_p = sem("s_cur"), sem("s_s_p"), sem("s_sq"), sem("s_p")
        s_o_p, s_on, s_onT_p, s_onT, s_y_p = sem("s_o_p"), sem("s_on"), sem("s_onT_p"), sem("s_onT"), sem("s_y_p")
        s_h1, s_q2, s_q2T_p, s_q2T, s_sc_p = sem("s_h1"), sem("s_q2"), sem("s_q2T_p"), sem("s_q2T"), sem("s_sc_p")
        s_topk, s_dif, s_ex = sem("s_topk"), sem("s_dif"), sem("s_ex")
        s_idx, s_res = sem("s_idx"), sem("s_res")
        s_rows = [sem(f"s_rows{c}") for c in range(PH)]
        s_x, s_g, s_vals, s_scaled, s_summed = sem("s_x"), sem("s_g"), sem("s_vals"), sem("s_scaled"), sem("s_summed")
        s_out = [sem(f"s_out{j}") for j in range(GATHERED)]
        s_lots, s_lots_p, s_scal = sem("s_lots"), sem("s_lots_p"), sem("s_scal")
        s_skip, s_resd, s_outd = sem("s_skip"), sem("s_resd"), sem("s_outd")
        s_hot, s_wgt_p, s_wgt = sem("s_hot"), sem("s_wgt_p"), sem("s_wgt")
        s_prod_p, s_gelu, s_weighed = sem("s_prod_p"), sem("s_gelu"), sem("s_weighed")
        s_table = [sem(f"s_table{n}") for n in range(WBUF)]
        s_sum_p = sem("s_sum_p")
        s_gathering, s_searching = sem("s_gathering"), sem("s_searching")
        s_dve = sem("s_dve")

        block = ctx.enter_context(nc.Block())

        def tile(i, j):
            return i * GATHERED + (2 + j)

        def quarters(i, j):
            if j == 0:
                return [(tile(i - 1, 1), 1, 2), (tile(i - 1, 1), 1, 3), (tile(i - 1, 2), 2, 0)]
            if j == 1:
                return [(tile(i - 1, 2), 2, q) for q in (1, 2, 3)]
            return [(tile(i, 0), 0, q) for q in (0, 1, 2)]

        def quarters_dense(i, first):
            own_quarters = [(tile(i - 1, 1), 1, 0), (tile(i - 1, 1), 1, 1)]
            return [None if first else (tile(i - 1, 0), 0, 3)] + own_quarters

        LAST = [(tile(GROUPS - 1, 0), 0, 3)] + [(tile(GROUPS - 1, j), j, q) for j in (1, 2) for q in range(QUARTERS)]

        @block.sync
        def _(sp):
            def load_txt(b, par):
                sp.dma_start(h0[:, par, :], txt[bass.ds(b, 1), :, :].rearrange("o n d -> (o n) d")).then_inc(s_txt[par], 16)

            def store_patch(g, j):
                for m in range(P // PATCHES):
                    sp.dma_start(out[g * (P // PATCHES) + m, 0:PATCHES, :],
                                 res[m * PATCHES:(m + 1) * PATCHES, j, :]).then_inc(s_out[j], 16)

            def store_txt(b, src, done):
                sp.dma_start(out[bass.ds(b, 1), PATCHES:PATCHES + TEXT, :].rearrange("o n d -> (o n) d"),
                             src).then_inc(done, 16)

            def stream_down(i, slices):
                for s in slices:
                    if s >= WBUF:
                        sp.wait_ge(s_prod_p, i * SLICES + (s - WBUF + 1))
                    elif s == 0:
                        sp.wait_ge(s_wgt_p, i * SLICES + SLICES)
                    sp.dma_start(wbuf[:, s % WBUF, :], down_t[s, :, :]).then_inc(s_table[s % WBUF], 16)

            def stream_up(i, slices):
                for s in slices:
                    if s >= WBUF:
                        sp.wait_ge(s_sum_p, i * SLICES + (s - WBUF + 1))
                    else:
                        sp.wait_ge(s_prod_p, (i + 1) * SLICES - (WBUF - s - 1))
                    sp.dma_start(wbuf[:, s % WBUF, :], up_t[s, :, :]).then_inc(s_table[s % WBUF], 16)

            def dense(i, first=False):
                if not first:
                    stream_up(i - 1, range(WBUF, SLICES))
                f = i * GROUP + 2
                sp.wait_ge(s_h1, f + 1)
                load_txt(f, 0)
                if not first:
                    sp.wait_ge(s_res, tile(i - 1, 0) + 1)
                    store_txt(i * GROUP - 3, res[:, 0, :], s_out[0])

            def gathered(i, j, first=False, last=False):
                if j == 2:
                    stream_down(i, range(WBUF, SLICES))
                if not last or j == 0:
                    f = i * GROUP + (3 + j)
                    sp.wait_ge(s_h1, f + 1)
                    load_txt(f, (3 + j) % 2)
                if j == 0 and not first:
                    sp.wait_ge(s_resd, i)
                    store_txt(i * GROUP - GROUP, resd[:], s_outd)
                if j < 2:
                    sp.wait_ge(s_res, tile(i - 1, 1 + j) + 1)
                    if first:
                        store_patch(j, 1 + j)
                    else:
                        store_txt(i * GROUP - 2 + j, res[:, 1 + j, :], s_out[1 + j])
                if j == 1:
                    stream_down(i, range(WBUF))
                if j == 2:
                    stream_up(i, range(WBUF))

            sp.dma_start(xpat, patches).then_inc(s_tok, 16)
            sp.dma_start(wtok, tok_w).then_inc(s_tok, 16)
            sp.dma_start(btok[:], tok_b).then_inc(s_tok, 16)
            sp.dma_start(bqf[:], bq).then_inc(s_ffn_w, 16)
            sp.dma_start(wqf, wq_ffn).then_inc(s_ffn_w, 16)
            sp.dma_start(keysT, keys).then_inc(s_ffn_w, 16)
            for f in range(2):
                sp.wait_ge(s_h1, f + 1)
                load_txt(f, f)
            dense(0, first=True)
            for j in range(GATHERED):
                gathered(0, j, first=True)
            dense(1)
            with sp.Fori(1, GROUPS - 1) as i:
                for j in range(GATHERED):
                    gathered(i, j)
                dense(i + 1)
            for j in range(GATHERED):
                gathered(GROUPS - 1, j, last=True)
            stream_up(GROUPS - 1, range(WBUF, SLICES))
            sp.wait_ge(s_resd, GROUPS)
            store_txt(BATCH - GROUP, resd[:], s_outd)
            for j in range(GATHERED):
                sp.wait_ge(s_res, tile(GROUPS - 1, j) + 1)
                store_txt(BATCH - GATHERED + j, res[:, j, :], s_out[j])
            sp.wait_ge(s_outd, 16 * GROUPS)
            sp.wait_ge(s_out[0], 16 * GROUPS)
            for j in (1, 2):
                sp.wait_ge(s_out[j], 16 * (GROUPS + P // PATCHES))

        @block.gpsimd
        def _(pool):
            pool_count = [0]

            def link(ins):
                pool_count[0] += 1
                ins.then_inc(s_pool, 1)
                pool.wait_ge(s_pool, pool_count[0])

            link(nc.gpsimd.memset(ident[:], 0.0))
            link(nc.gpsimd.affine_select(out=ident[:], in_=ident[:], compare_op=ALU.not_equal, fill=1.0, base=0,
                                         pattern=[[-1, P]], channel_multiplier=1))
            link(nc.gpsimd.memset(tri[:], 1.0))
            link(nc.gpsimd.affine_select(out=tri[:], in_=tri[:], compare_op=ALU.is_ge, fill=0.0, base=0,
                                         pattern=[[1, P]], channel_multiplier=-1))
            blocks = blk[:].rearrange("p (b j) -> p b j", j=PATCHES)
            tris = tri[:].rearrange("p (b j) -> p b j", j=PATCHES)
            link(nc.gpsimd.affine_select(out=blocks, in_=tris, compare_op=ALU.is_ge, fill=0.0, base=0,
                                         pattern=[[-PATCHES, P // PATCHES], [0, PATCHES]], channel_multiplier=1))
            link(nc.gpsimd.affine_select(out=blocks, in_=blocks, compare_op=ALU.is_ge, fill=0.0, base=PATCHES - 1,
                                         pattern=[[PATCHES, P // PATCHES], [0, PATCHES]], channel_multiplier=-1))
            link(nc.gpsimd.memset(own[:], 0.0))
            for r in range(3):
                link(nc.gpsimd.affine_select(out=own[:], in_=own[:], compare_op=ALU.not_equal, fill=1.0,
                                             base=-2 * PH * r, pattern=[[-1, 2 * PH]], channel_multiplier=1))
            nc.gpsimd.iota(number[:], pattern=[[1, P]], base=0, channel_multiplier=0,
                           allow_small_or_imprecise_dtypes=True).then_inc(s_const, 1)

            def gather(t, j, first=False):
                pool.wait_ge(s_idx, t + 1)
                for c in range(PH):
                    if c % 2 == 0 and not first:
                        pool.wait_ge(s_summed, (t - 1) * QUARTERS + (c // 2 + 1))
                        pool.sem_inc(s_gathering, 1)
                    for k in range(c * K, (c + 1) * K):
                        nc.gpsimd.indirect_dma_start(
                            rows[:, k, :], None, table,
                            bass.IndirectOffsetOnAxis(ap=idx[:, j, k:k + 1], axis=0)).then_inc(s_rows[c], 16)

            gather(0, 1, first=True)
            gather(1, 2)
            with pool.Fori(0, GROUPS) as i:
                for j in range(GATHERED):
                    gather(tile(i, j), j)

        PRODUCTS = [6, 2, 6, 0, 8, 2, 2, 6]
        WEIGHED = [2, 4, 6, 0, 6, 4, 4, 6]
        SUM = [6, 4, 4, 0, 6, 2, 2, 8]
        WEIGHTS = [[2, 2, 4, 0, 4, 0, 0, 4], [4, 2, 4, 0, 4, 0, 0, 2]]
        HOTS = [[3, 3, 3, 0, 4, 1, 1, 3], [3, 3, 3, 0, 5, 0, 0, 0]]
        NOTHING = [lambda: None] * 8

        def spread(kind, i, counts, start=0, **how):
            out_ = []
            for n in counts:
                out_.append(lambda part=range(start, start + n): kind(i, part, **how))
                start += n
            return out_

        @block.scalar
        def _(act):
            act.dma_start(wqk_in[:, 0, 0:D], w_q).then_inc(s_attn_w, 16)
            act.dma_start(wqk_in[:, 0, D:2 * D], w_kv[:, 0:D]).then_inc(s_attn_w, 16)
            act.dma_start(wv[:], w_kv[:, D:2 * D]).then_inc(s_attn_w, 16)
            act.dma_start(wout[:], w_out).then_inc(s_attn_w, 16)

            def gelu(t, q):
                act.wait_ge(s_x, t * QUARTERS + (q + 1))
                nc.scalar.activation(g[:, q * CH:(q + 1) * CH], x[:, q * CH:(q + 1) * CH],
                                     ACT.Gelu_apprx_tanh).then_inc(s_g, 1)

            def scale_up(t, q, first=0, last=CH):
                act.wait_ge(s_vals, t * QUARTERS + (q + 1))
                for k in range(q * CH + first, q * CH + last):
                    up = rows[:, k, D:2 * D]
                    ins = nc.scalar.activation(up, up, ACT.Copy, scale=vals[:, k:k + 1])
                    if k % 4 == 3:
                        ins.then_inc(s_scaled, 1)

            def copy_weights(i, slices):
                for s in slices:
                    act.wait_ge(s_wgt_p, i * SLICES + (s + 1))
                    nc.scalar.copy(gd_h[:, :, :, TP * s:TP * s + TP],
                                   X[:, s % 2, :].rearrange("p (n h j) -> p j h n", n=TP, h=2)).then_inc(s_wgt, 1)

            def gelu_dense(i, slices):
                for s in slices:
                    act.wait_ge(s_prod_p, i * SLICES + (s + 1))
                    if s >= GELU_BUF:
                        act.wait_ge(s_weighed, i * SLICES + (s - GELU_BUF + 1))
                    nc.scalar.activation(act_x[:, s % GELU_BUF, :], X[:, s % 2, :], ACT.Gelu_apprx_tanh).then_inc(s_gelu, 1)

            def project(f, patch=None, b=None, fill=NOTHING):
                act.wait_ge(s_xnT_p, f + 1)
                nc.scalar.copy(xnT[:], B[:, 0:P]).then_inc(s_xnT, 1)
                if patch is None:
                    nc.scalar.copy(cur[:].rearrange("p a j -> p (a j)"),
                                   keep[:, bass.ds(b, 1), :, :].rearrange("p o a j -> p (o a j)")).then_inc(s_cur, 1)
                fill[5]()
                act.wait_ge(s_qk_p, f + 1)
                nc.scalar.copy(qkT[:].rearrange("p g n -> p (g n)"), B[:]).then_inc(s_qk, 1)
                if patch is not None:
                    act.wait_ge(s_qk, f + 1)
                    act.wait_ge(s_xnT, f + 1)
                    mine = keep[:, patch * 8:(patch + 1) * 8, :, :]
                    for n in range(HG):
                        nc.scalar.copy(mine[:, :, n, :], qkT[:, HG + n, :].rearrange("p (b j) -> p b j", j=PATCHES))
                    nc.scalar.copy(mine[:, :, 2, :],
                                   xnT[:].rearrange("p (b j) -> p b j", j=PATCHES)).then_inc(s_cur, 1)
                fill[6]()

            def step(f, three, patch=None, dense=None, work=NOTHING, ahead=None):
                if three[0]:
                    gelu(three[0][0], three[0][2])
                act.wait_ge(s_s_p, f + 1)
                ins = nc.scalar.activation(pT[:].rearrange("p (l g) n -> p l (g n)", g=HG), A[:, :, 0:HG * P],
                                           ACT.Square, bias=1.0, scale=QSCALE)
                if patch is None:
                    ins = nc.scalar.activation(pTp.rearrange("p (l g) n -> p l (g n)", g=HG),
                                               A[0:PATCHES, :, HG * P:2 * HG * P], ACT.Square, bias=1.0, scale=QSCALE)
                ins.then_inc(s_sq, 1)
                work[0]()
                if three[0]:
                    scale_up(three[0][0], three[0][2])
                work[1]()
                act.wait_ge(s_onT_p, f + 1)
                nc.scalar.copy(onT[:], B[:, 0:P]).then_inc(s_onT, 1)
                if three[1]:
                    gelu(three[1][0], three[1][2])
                work[2]()
                act.wait_ge(s_q2T_p, f + 1)
                nc.scalar.copy((q2T if dense is None else q2Td)[:], B[:, 2 * P:3 * P]).then_inc(s_q2T, 1)
                work[3]()
                if three[1]:
                    scale_up(three[1][0], three[1][2])
                work[4]()
                if three[2]:
                    gelu(three[2][0], three[2][2])
                if ahead:
                    project(*ahead, fill=work)
                else:
                    work[5]()
                    work[6]()
                if dense is None and three[2]:
                    scale_up(three[2][0], three[2][2])
                    work[7]()
                act.wait_ge(s_dif, f + 1)
                nc.scalar.activation(ex[:], dif[:], ACT.Exp).then_inc(s_ex, 1)
                if dense is not None and three[2]:
                    scale_up(three[2][0], three[2][2])
                if dense is not None:
                    act.wait_ge(s_lots_p, dense + 1)
                    for n in range(2):
                        r = slice(n * NK, (n + 1) * NK)
                        lots_t = B[r, 0:3 * P].rearrange("p (a n) -> p a n", a=3)[:, :, r]
                        nc.scalar.copy(scal[r, 0:2, :], lots_t[:, 0:2, :])
                        ins = nc.scalar.copy(scal[r, 2 + n, :], lots_t[:, 2, :])
                    ins.then_inc(s_scal, 1)

            def dense_step(i, first=False):
                step(i * GROUP + 2, quarters_dense(i, first), dense=i,
                     ahead=(i * GROUP + 3, None, i * GROUP + 1))

            def gathered_step(i, j, last=False):
                work = [spread(copy_weights, i, WEIGHTS[0]), spread(copy_weights, i, WEIGHTS[1], sum(WEIGHTS[0])),
                        spread(gelu_dense, i, PRODUCTS)][j]
                step(i * GROUP + (3 + j), quarters(i, j), work=work,
                     ahead=None if last else (i * GROUP + (4 + j), None, i * GROUP + (2 + j)))

            act.wait_ge(s_fold, 1)
            nc.scalar.copy(mt[:].rearrange("p c n -> p (c n)"), A[:].rearrange("p a n -> p (a n)")).then_inc(s_fold_c, 1)
            project(0, patch=0)
            step(0, [None] * 3, patch=0, ahead=(1, 1))
            step(1, [None] * 3, patch=1, ahead=(2, None, 0))
            dense_step(0, first=True)
            for j in range(GATHERED):
                gathered_step(0, j)
            dense_step(1)
            with act.Fori(1, GROUPS - 1) as i:
                for j in range(GATHERED):
                    gathered_step(i, j)
                dense_step(i + 1)
            for j in range(GATHERED):
                gathered_step(GROUPS - 1, j, last=j == GATHERED - 1)
            for t, j, q in LAST:
                gelu(t, q)
                scale_up(t, q)

        @block.vector
        def _(dve):
            count = [0]

            def link(ins):
                count[0] += 1
                ins.then_inc(s_dve, 1)
                dve.wait_ge(s_dve, count[0])

            def clear():
                dve.sem_clear(s_dve)
                count[0] = 0

            def layernorm(dst, src, done):
                link(nc.vector.bn_stats(stats[:], src))
                link(nc.vector.bn_aggr(mv[:], stats[:]))
                link(nc.vector.tensor_scalar(yt[:], mv[:, 1:2], EPS, None, ALU.add))
                link(nc.vector.tensor_scalar(bits[:], yt[:].bitcast(I32), 1, None, ALU.logical_shift_right))
                nc.vector.tensor_scalar(y[:].bitcast(I32), bits[:], -1.0, RSQRT_SEED, ALU.mult, ALU.add)
                link(nc.vector.tensor_scalar(hv[:], yt[:], -0.5, None, ALU.mult))
                for _ in range(NEWTON):
                    link(nc.vector.scalar_tensor_tensor(yt[:], y[:], hv[:], y[:], ALU.mult, ALU.mult))
                    link(nc.vector.scalar_tensor_tensor(y[:], yt[:], 1.5, y[:], ALU.add, ALU.mult))
                nc.vector.tensor_scalar(dst, src, mv[:, 0:1], y[:], ALU.subtract, ALU.mult).then_inc(done, 1)

            def dots(t, j, q):
                for k in range(q * CH, (q + 1) * CH):
                    if k % K == 0:
                        dve.wait_ge(s_rows[k // K], t * (16 * K) + 16 * K)
                    last = nc.vector.tensor_tensor_reduce(rows[:, k, 0:D], rows[:, k, 0:D], qin[:, j, :], 1.0, 0.0,
                                                          ALU.mult, ALU.add, x[:, k:k + 1])
                last.then_inc(s_x, 1)

            def factors(t, j, q):
                part = slice(q * CH, (q + 1) * CH)
                dve.wait_ge(s_g, t * QUARTERS + (q + 1))
                nc.vector.tensor_tensor(vals[:, part], g[:, part], wts[:, j, part], ALU.mult).then_inc(s_vals, 1)

            def result(i, j, stored=True):
                dve.wait_ge(s_summed, tile(i, j) * QUARTERS + QUARTERS)
                if stored:
                    dve.wait_ge(s_out[j], i * 16 + (0 if j == 0 else 16 * (P // PATCHES)))
                nc.vector.tensor_reduce(res[:, j, :], ACC[:].rearrange("p a d -> p d a"), AX_X,
                                        ALU.add).then_inc(s_res, 1)

            def search(f, write, between, middle, later):
                for a in range(4):
                    dve.wait_ge(s_sc_p, f * 4 + (a + 1))
                    dve.sem_inc(s_searching, 1)
                    for n in range(4 * a, 4 * a + 4):
                        last = nc.vector.max(top[:, 0, n // PH, n % PH, :], A[:, a, (n % 4) * E:(n % 4 + 1) * E])
                link(last)
                for n in range(2 * PH):
                    last = nc.vector.max_index(top_i[:, n // PH, n % PH, :], top[:, 0, n // PH, n % PH, :],
                                               A[:, n // 4, (n % 4) * E:(n % 4 + 1) * E])
                last.then_inc(s_topk, 1)
                between()
                dve.wait_ge(s_topk, f + 1)
                nc.vector.tensor_scalar(top[:, 1, 0, :, :], top_i[:, 0, :, :], float(E), None, ALU.mult)
                link(nc.vector.tensor_copy(top[:, 1, 1, :, :], top_i[:, 1, :, :]))
                at = 0
                for a, nb in [(a, K // (a + 1)) for a in range(4)]:
                    nc.vector.tensor_tensor(
                        cand[:, :, :, at:at + nb],
                        top[:, :, 0, :, a:a + 1].to_broadcast([P, 2, PH, nb]), top[:, :, 1, :, 0:nb], ALU.add)
                    at += nb
                link(nc.vector.tensor_tensor(cand[:, :, :, at:NC], top[:, :, 0, :, 4:K],
                                             top[:, :, 1, :, 0:1].to_broadcast([P, 2, PH, K - 4]), ALU.add))
                for h in range(PH):
                    last = nc.vector.max(best[:, h, :], cand[:, 0, h, :])
                link(last)
                middle()
                for h in range(PH):
                    last = nc.vector.max_index(best_p[:, h, :], best[:, h, :], cand[:, 0, h, :])
                link(last)
                link(nc.vector.tensor_copy(best_f[:], best_p[:].rearrange("p h k -> p (h k)")))
                link(nc.vector.tensor_tensor(hit[:], best_f[:].unsqueeze(2).to_broadcast([P, NK, NC]),
                                             number[:, 0:NC].unsqueeze(1).to_broadcast([P, NK, NC]), ALU.is_equal))
                hits = hit[:].rearrange("p (h k) n -> p h k n", k=K)
                link(nc.vector.tensor_tensor(hits, hits, cand[:, 1, :, :].unsqueeze(2).to_broadcast([P, PH, K, NC]),
                                             ALU.mult))
                link(nc.vector.tensor_reduce(best_f[:], hit[:], AX_X, ALU.add))
                later()
                write()
                nc.vector.tensor_tensor(dif[:], best[:], best[:, :, 0:1].to_broadcast([P, PH, K]),
                                        ALU.subtract).then_inc(s_dif, 1)

            def softmax(f, dst):
                dve.wait_ge(s_ex, f + 1)
                link(nc.vector.tensor_reduce(sm[:], ex[:], AX_X, ALU.add))
                link(nc.vector.reciprocal(sm[:], sm[:]))
                link(nc.vector.tensor_tensor(dst.rearrange("p (h k) -> p h k", k=K), ex[:],
                                             sm[:].unsqueeze(2).to_broadcast([P, PH, K]), ALU.mult))

            def one_hots(i, slices, first=False):
                for s in slices:
                    if s == 0:
                        dve.wait_ge(s_scal, i + 1)
                    if s >= HOTS_BUF or not first:
                        dve.wait_ge(s_wgt_p, i * SLICES + (s - HOTS_BUF + 1))
                    buf, cols = s % HOTS_BUF, slice(TP * s, TP * s + TP)
                    link(nc.vector.tensor_tensor(
                        hot_ij[:, buf, :, :, :], number[:].unsqueeze(1).unsqueeze(1).to_broadcast([P, 2, TP, E]),
                        scal[:, 0:2, cols].unsqueeze(3).to_broadcast([P, 2, TP, E]), ALU.is_equal))
                    nc.vector.tensor_tensor(
                        hot_w[:, buf, :, :, :], hot_ij[:, buf, 1, :, :].unsqueeze(2).to_broadcast([P, TP, 2, E]),
                        scal[:, 2:4, cols].rearrange("p h n -> p n h").unsqueeze(3).to_broadcast([P, TP, 2, E]),
                        ALU.mult).then_inc(s_hot, 1)

            def weigh(i, slices):
                for s in slices:
                    dve.wait_ge(s_gelu, i * SLICES + (s + 1))
                    part = gd[:, s * SL * P:(s + 1) * SL * P]
                    nc.vector.tensor_tensor(part, part, act_x[:, s % GELU_BUF, :], ALU.mult).then_inc(s_weighed, 1)

            def normalize(f, par, patch=None):
                src = h0[:, par, :]
                if patch is not None:
                    dve.wait_ge(s_emb, f + 1)
                    link(nc.vector.tensor_copy(src, B[:, 3 * P:4 * P]))
                else:
                    dve.wait_ge(s_txt[par], (f - par) * 8)
                layernorm(xn[:], src, s_xn)

            def values(f, patch=None):
                dve.wait_ge(s_v_p, f + 1)
                last = nc.vector.tensor_copy(va[:, :, 0:DH], B[:, 0:P].rearrange("p (h j) -> p h j", j=DH))
                if patch is None:
                    last = nc.vector.tensor_copy(vpa[:, :, 0:DH],
                                                 B[0:PATCHES, P:2 * P].rearrange("p (h j) -> p h j", j=DH))
                last.then_inc(s_v, 1)

            def step(f, par, j, three, patch=None, dense=None, hots=NOTHING, weighs=NOTHING, ahead=None,
                     before=None, at_start=None, before_search=None, at_end=None):
                src = h0[:, par, :]
                if patch == 0:
                    dve.wait_ge(s_fold, 2)
                    nc.vector.tensor_copy(bias[:, 0:PH], X[:, 0, 0:PH])
                    link(nc.vector.tensor_copy(bias[:, PH:2 * PH], X[:, 1, 0:PH]))
                    for r in range(2):
                        link(nc.vector.tensor_copy(bparts[:, r, :], bias[:]))
                        link(nc.vector.tensor_tensor(bias[:], bias[:], bparts[:, r, :], ALU.subtract))
                    nc.vector.tensor_copy(bparts[:, 2, :], bias[:]).then_inc(s_bias_split, 1)
                if three[0]:
                    dots(*three[0])
                if before is not None:
                    softmax(f - 1, wts[:, before, :])
                hots[0]()
                if at_start:
                    at_start()
                dve.wait_ge(s_sq, f + 1)
                mask = (tri if patch is None else blk)[:].unsqueeze(1).to_broadcast([P, H, P])
                last = nc.vector.scalar_tensor_tensor(pT[:], pT[:], 1.0, mask, ALU.add, ALU.mult)
                if patch is None:
                    last = nc.vector.tensor_scalar(pTp, pTp, 1.0, None, ALU.add)
                last.then_inc(s_p, 1)
                if three[0]:
                    factors(*three[0])
                weighs[0]()
                if patch == 0:
                    dve.wait_ge(s_fold, 3)
                    nc.vector.tensor_tensor(
                        brows[:], X[0:3 * 2 * PH, 0:1, 0:E].to_broadcast([3 * 2 * PH, 2 * PH, E]),
                        own[:].unsqueeze(2).to_broadcast([3 * 2 * PH, 2 * PH, E]), ALU.mult).then_inc(s_bias, 1)
                if three[1]:
                    dots(*three[1])
                dve.wait_ge(s_o_p, f + 1)
                o = B[:, 2 * P:2 * P + H * (DH + 1)].rearrange("p (h j) -> p h j", j=DH + 1)
                link(nc.vector.tensor_scalar(rden[:].unsqueeze(2), o[:, :, DH:DH + 1], 2 * EPS, None, ALU.max))
                link(nc.vector.reciprocal(rden[:], rden[:]))
                nc.vector.tensor_tensor(on[:], o[:, :, 0:DH], rden[:].unsqueeze(2).to_broadcast([P, H, DH]),
                                        ALU.mult).then_inc(s_on, 1)
                hots[1]()
                weighs[1]()
                if three[1]:
                    factors(*three[1])
                resid = h1d[:] if dense is not None else h1[:, j, :]
                if dense is not None and three[0]:
                    dve.wait_ge(s_skip, dense)
                dve.wait_ge(s_y_p, f + 1)
                nc.vector.tensor_tensor(resid, src, B[:, P:2 * P], ALU.add).then_inc(s_h1, 1)
                dve.wait_ge(s_h1, f + 1)
                layernorm(q2[:], resid, s_q2)
                if dense is None:
                    dve.wait_ge(s_q2, f + 1)
                    nc.vector.tensor_copy(qin[:, j, :], q2[:])
                hots[2]()
                weighs[2]()
                if before_search:
                    before_search()
                if ahead:
                    normalize(*ahead)
                if three[2]:
                    dots(*three[2])

                def between():
                    hots[4]()
                    weighs[4]()
                    if three[2]:
                        factors(*three[2])

                def middle():
                    hots[5]()
                    weighs[5]()

                def later():
                    hots[6]()
                    weighs[6]()

                if dense is None:
                    search(f, lambda: nc.vector.tensor_copy(idx[:, j, :], best_f[:]).then_inc(s_idx, 1),
                           between, middle, later)
                else:
                    def split():
                        link(nc.vector.tensor_copy(best_p[:].rearrange("p h k -> p (h k)"), best_f[:]))
                        number_i = best_p[:].rearrange("p h k -> p (h k)").bitcast(I32)
                        nc.vector.tensor_scalar(ij[:, 0, :], number_i, E.bit_length() - 1, None, ALU.logical_shift_right)
                        link(nc.vector.tensor_scalar(ij[:, 1, :], number_i, E - 1, None, ALU.bitwise_and))
                        nc.vector.tensor_copy(lots[:, 0:2, :, :], ij[:].unsqueeze(2).to_broadcast([P, 2, 2, NK]))

                    search(f, split, between, middle, later)
                    softmax(f, wtd[:])
                    nc.vector.tensor_copy(lots[:, 2, :, :],
                                          wtd[:].unsqueeze(1).to_broadcast([P, 2, NK])).then_inc(s_lots, 1)
                if ahead:
                    values(ahead[0], ahead[2])
                hots[7]()
                weighs[7]()
                if at_end:
                    at_end()
                clear()

            def result_dense(i):
                dve.wait_ge(s_sum_p, i * SLICES + SLICES)
                nc.vector.tensor_copy(resd[:], X[:, 0, 0:D]).then_inc(s_resd, 1)

            def dense_step(i, first=False, second=False):
                step(i * GROUP + 2, 0, None, quarters_dense(i, first), dense=i,
                     ahead=(i * GROUP + 3, 1, None), before=GATHERED - 1,
                     before_search=None if first else lambda: result(i - 1, 0, not second),
                     at_start=None if first or second else lambda: dve.wait_ge(s_outd, (i - 1) * 16))

            def gathered_step(i, j, first=False, last=False):
                step(i * GROUP + (3 + j), (3 + j) % 2, j, quarters(i, j),
                     before=j - 1 if j else None,
                     hots=[spread(one_hots, i, HOTS[0], first=first), spread(one_hots, i, HOTS[1], sum(HOTS[0]), first=first),
                           NOTHING][j],
                     weighs=spread(weigh, i, WEIGHED) if j == 2 else NOTHING,
                     ahead=None if last else (i * GROUP + (4 + j), (4 + j) % 2, None),
                     at_start=[None if first else lambda: result_dense(i - 1), None,
                               lambda: result(i - 1, 2, not first)][j],
                     at_end=(lambda: result(i - 1, 1, not first)) if j == 0 else None)

            nc.vector.memset(ones[:], 1.0)
            nc.vector.memset(ones_b[:], 1.0).then_inc(s_ones, 1)
            nc.vector.memset(va[:], 1.0)
            nc.vector.memset(vpa[:], 1.0)
            nc.vector.memset(scal[:], 0.0)
            link(nc.vector.memset(wqk[:], 0.0))
            dve.wait_ge(s_attn_w, 64)
            nc.vector.tensor_copy(wqk[:].rearrange("p a g l j -> p (a g l) j")[:, :, 0:DH],
                                  wqk_in.rearrange("p o (a j) -> p (o a) j", j=DH)).then_inc(s_wqk, 1)
            dve.wait_ge(s_const, 1)
            nc.vector.tensor_copy(ident_b[:], ident[:]).then_inc(s_ones, 1)
            normalize(0, 0, 0)
            values(0, 0)
            step(0, 0, 1, [None] * 3, patch=0, ahead=(1, 1, 1))
            step(1, 1, 2, [None] * 3, patch=1, ahead=(2, 0, None), before=1)
            dense_step(0, first=True)
            for j in range(GATHERED):
                gathered_step(0, j, first=True)
            dense_step(1, second=True)
            with dve.Fori(1, GROUPS - 1) as i:
                for j in range(GATHERED):
                    gathered_step(i, j)
                dense_step(i + 1)
            for j in range(GATHERED):
                gathered_step(GROUPS - 1, j, last=j == GATHERED - 1)
            softmax(TILES - 1, wts[:, GATHERED - 1, :])
            i = GROUPS - 1
            for n in range(len(LAST)):
                dots(*LAST[n])
                factors(*LAST[n])
                if n == 0:
                    result(i, 0)
                if n == 2:
                    dve.wait_ge(s_outd, i * 16)
                    result_dense(i)
                if n == 4:
                    result(i, 1)
            result(i, 2)

        @block.tensor
        def _(pe):
            mm = nc.tensor.matmul

            def fold_keys():
                pe.wait_ge(s_ffn_w, 48)
                for c in range(2):
                    r = slice(c * HALF, (c + 1) * HALF)
                    for h in range(PH):
                        last = mm(A[:, 2 * c + h // 4, (h % 4) * E:(h % 4 + 1) * E], wqf[r, h, :], keysT[r, h, :],
                                  start=True, stop=True)
                last.then_inc(s_fold, 1)

            def fold_bias():
                for c in range(2):
                    r = slice(c * HALF, (c + 1) * HALF)
                    for h in range(PH):
                        last = mm(X[:, c, h:h + 1], keysT[r, h, :], bqf[r, h:h + 1], start=True, stop=True)
                last.then_inc(s_fold, 1)

            def turn_bias():
                pe.wait_ge(s_bias_split, 1)
                pe.wait_ge(s_ones, 2)
                mm(X[0:3 * 2 * PH, 0, 0:E], bparts[:].rearrange("p r n -> p (r n)"), ident_b[:], start=True,
                   stop=True).then_inc(s_fold, 1)

            def sum_up(t, j, q, first=False):
                group = CH // 4
                if q == 0 and not first:
                    pe.wait_ge(s_res, t)
                for n in range(q * group, (q + 1) * group):
                    pe.wait_ge(s_scaled, t * (NK // 4) + (n + 1))
                    last = mm(ACC[:], ident[:], rows[:, 4 * n:4 * n + 4, D:2 * D], start=n == 0,
                              stop=n == NK // 4 - 1)
                    if n == 0:
                        mm(ACC[:, 0, :], ident[:], h1[:, j, :], start=False, stop=False)
                last.then_inc(s_summed, 1)

            def table(i, s, base):
                pe.wait_ge(s_table[s % WBUF], i * (2 * SLICES // WBUF * 16) + (base // WBUF + s // WBUF + 1) * 16)
                return wbuf[:, s % WBUF, :].rearrange("p (j n) -> p j n", n=P)

            def weights(i, slices, first=False):
                for s in slices:
                    pe.wait_ge(s_hot, i * SLICES + (s + 1))
                    if s >= 2:
                        pe.wait_ge(s_wgt, i * SLICES + (s - 1))
                    elif not first:
                        pe.wait_ge(s_resd, i)
                    for n in range(TP):
                        last = mm(X[:, s % 2, n * 2 * P:(n + 1) * 2 * P], hot_ij[:, s % HOTS_BUF, 0, n, :],
                                  hot_w[:, s % HOTS_BUF, n, :, :].rearrange("p h e -> p (h e)"), start=True, stop=True)
                    last.then_inc(s_wgt_p, 1)

            def products(i, slices):
                for s in slices:
                    w = table(i, s, 0)
                    if s >= 2:
                        pe.wait_ge(s_gelu, i * SLICES + (s - 1))
                    else:
                        pe.wait_ge(s_wgt, i * SLICES + (SLICES - 1 + s))
                    for n in range(SL):
                        last = mm(X[:, s % 2, n * P:(n + 1) * P], w[:, n, :], q2Td[:], start=True, stop=True)
                    last.then_inc(s_prod_p, 1)

            def sums(i, slices):
                for s in slices:
                    w = table(i, s, SLICES)
                    if s == 0:
                        pe.wait_ge(s_weighed, i * SLICES + SLICES)
                        mm(X[:, 0, 0:D], ident[:], h1d[:], start=True, stop=False).then_inc(s_skip, 1)
                    for n in range(SL):
                        last = mm(X[:, 0, 0:D], gd_j[:, s * SL + n, :], w[:, n, :], start=False,
                                  stop=s * SL + n == E - 1)
                    last.then_inc(s_sum_p, 1)

            def project(f, patch=None, fill=NOTHING):
                if patch is not None:
                    for c in range(PC):
                        mm(B[:, 3 * P:4 * P], xpat[:, c, patch * P:(patch + 1) * P], wtok[:, c, :],
                           start=c == 0, stop=False)
                    mm(B[:, 3 * P:4 * P], ones[:], btok[:], start=False, stop=True).then_inc(s_emb, 1)
                if patch == 0:
                    fold_keys()
                pe.wait_ge(s_xn, f + 1)
                nc.tensor.transpose(B[:, 0:P], xn[:], ident[:]).then_inc(s_xnT_p, 1)
                fill[5]()
                pe.wait_ge(s_xnT, f + 1)
                for n in range(2 * HG):
                    last = mm(B[:, n * P:(n + 1) * P], wqk[:, n // HG, n % HG, :, :].rearrange("p l j -> p (l j)"),
                              xnT[:], start=True, stop=True)
                last.then_inc(s_qk_p, 1)
                fill[6]()
                if patch == 0:
                    fold_bias()
                    pe.wait_ge(s_fold_c, 1)
                pe.wait_ge(s_qk, f + 1)
                last = mm(B[:, 0:P], xnT[:], wv[:], start=True, stop=True)
                if patch is None:
                    pe.wait_ge(s_cur, f + 1)
                    last = mm(B[0:PATCHES, P:2 * P], cur[:, 2, :], wv[:], start=True, stop=True)
                last.then_inc(s_v_p, 1)

            def step(f, three, work, patch=None, dense=None, ahead=None, before_output=None):
                if patch != 0:
                    pe.wait_ge(s_topk, f)
                for h in range(H):
                    l, n = h % HL, h // HL
                    r = slice(32 * l, 32 * l + DH)
                    last = mm(A[:, l, n * P:(n + 1) * P], qkT[r, HG + n, :], qkT[r, n, :], start=True, stop=True)
                    if patch is None:
                        last = mm(A[0:PATCHES, l, (HG + n) * P:(HG + n + 1) * P], cur[r, n, :], qkT[r, n, :],
                                  start=True, stop=True)
                last.then_inc(s_s_p, 1)
                if patch == 0:
                    turn_bias()
                work[0]()
                pe.wait_ge(s_v, f + 1)
                pe.wait_ge(s_p, f + 1)
                if before_output:
                    before_output()
                for h in range(H):
                    l, n = h % HL, h // HL
                    to = B[:, 2 * P + h * (DH + 1):2 * P + (h + 1) * (DH + 1)]
                    last = mm(to, pT[:, l * HG + n, :], va[:, h, :], start=True, stop=patch is not None)
                    if patch is None:
                        last = mm(to, pTp[:, l * HG + n, :], vpa[:, h, :], start=False, stop=True)
                last.then_inc(s_o_p, 1)
                work[1]()
                pe.wait_ge(s_on, f + 1)
                nc.tensor.transpose(B[:, 0:P], on[:].rearrange("p h j -> p (h j)"), ident[:]).then_inc(s_onT_p, 1)
                pe.wait_ge(s_onT, f + 1)
                mm(B[:, P:2 * P], onT[:], wout[:], start=True, stop=True).then_inc(s_y_p, 1)
                if three[0]:
                    sum_up(*three[0])
                work[2]()
                pe.wait_ge(s_q2, f + 1)
                nc.tensor.transpose(B[:, 2 * P:3 * P], q2[:], ident[:]).then_inc(s_q2T_p, 1)
                work[3]()
                pe.wait_ge(s_q2T, f + 1)
                if patch == 0:
                    pe.wait_ge(s_bias, 1)
                inputs = q2T if dense is None else q2Td
                for a in range(4):
                    mm(A[:, a, :], inputs[:], mt[:, a // 2, (a % 2) * 512:(a % 2 + 1) * 512], start=True, stop=False)
                    mm(A[:, a, :], ones_b[:], brows[:, 4 * a:4 * a + 4, :].rearrange("p n e -> p (n e)"), start=False,
                       stop=True).then_inc(s_sc_p, 1)
                if three[1]:
                    sum_up(*three[1])
                work[4]()
                if ahead:
                    project(*ahead, fill=work)
                else:
                    work[5]()
                    work[6]()
                work[7]()
                if three[2]:
                    sum_up(*three[2])
                if dense is not None:
                    pe.wait_ge(s_v, f + 2)
                    pe.wait_ge(s_lots, dense + 1)
                    for n in range(3):
                        last = nc.tensor.transpose(B[:, n * P:(n + 1) * P], lots[:, n, :, :].rearrange("p a n -> p (a n)"),
                                                   ident[:])
                    last.then_inc(s_lots_p, 1)

            def dense_step(i, first=False):
                three = quarters_dense(i, first)
                if first:
                    three[1] = (*three[1], True)
                step(i * GROUP + 2, three, NOTHING if first else spread(sums, i - 1, SUM), dense=i,
                     ahead=(i * GROUP + 3,))

            def gathered_step(i, j, first=False, last=False):
                work = [spread(weights, i, WEIGHTS[0], first=first), spread(weights, i, WEIGHTS[1], sum(WEIGHTS[0])),
                        spread(products, i, PRODUCTS)][j]
                step(i * GROUP + (3 + j), quarters(i, j), work, ahead=None if last else (i * GROUP + (4 + j),),
                     before_output=(lambda: pe.wait_ge(s_scal, i + 1)) if j == 0 else None)

            pe.wait_ge(s_const, 1)
            pe.wait_ge(s_wqk, 1)
            pe.wait_ge(s_ones, 1)
            pe.wait_ge(s_tok, 48)
            project(0, 0)
            step(0, [None] * 3, NOTHING, patch=0, ahead=(1, 1))
            step(1, [None] * 3, NOTHING, patch=1, ahead=(2,))
            dense_step(0, first=True)
            for j in range(GATHERED):
                gathered_step(0, j, first=True)
            dense_step(1)
            with pe.Fori(1, GROUPS - 1) as i:
                for j in range(GATHERED):
                    gathered_step(i, j)
                dense_step(i + 1)
            for j in range(GATHERED):
                gathered_step(GROUPS - 1, j, last=j == GATHERED - 1)
            sums(GROUPS - 1, range(SLICES // 2))
            sum_up(*LAST[0])
            sums(GROUPS - 1, range(SLICES // 2, SLICES))
            for n in range(1, len(LAST)):
                sum_up(*LAST[n])


def kernel(x, txt, L0_tok_W, L0_tok_b, L0_attn_w_q, L0_attn_w_kv, L0_attn_w_out, L0_ffn_Wq, L0_ffn_bq,
           L0_ffn_keys, L0_ffn_w_down_embed, L0_ffn_w_up_embed):
    import numpy as np
    import concourse.bacc as bacc
    from concourse.bass_utils import run_bass_kernel_spmd

    con = np.ascontiguousarray
    side = 4
    pat = np.asarray(x).reshape(BATCH, 3, side, 16, side, 16).transpose(1, 3, 5, 0, 2, 4)
    pat = con(pat.reshape(PC, P, BATCH * PATCHES).transpose(1, 0, 2))
    arrays = {
        "patches": pat,
        "txt": con(txt),
        "tok_w": con(np.asarray(L0_tok_W).T.reshape(PC, P, D).transpose(1, 0, 2)),
        "tok_b": con(np.asarray(L0_tok_b).reshape(1, D)),
        "w_q": con(L0_attn_w_q),
        "w_kv": con(L0_attn_w_kv),
        "w_out": con(L0_attn_w_out),
        "wq_ffn": con(np.asarray(L0_ffn_Wq).reshape(PH, P, D).transpose(1, 0, 2)),
        "bq": con(np.asarray(L0_ffn_bq).reshape(PH, P).T),
        "keys": con(np.asarray(L0_ffn_keys).transpose(1, 3, 0, 2).reshape(P, PH, E)),
        "table": con(np.concatenate([L0_ffn_w_down_embed, L0_ffn_w_up_embed], axis=1)),
        "down_t": con(np.asarray(L0_ffn_w_down_embed).reshape(E, SLICES, SL, D).transpose(1, 3, 2, 0)
                      .reshape(SLICES, D, SL * E)),
        "up_t": con(np.asarray(L0_ffn_w_up_embed).reshape(E, SLICES, SL, D).transpose(1, 0, 2, 3)
                    .reshape(SLICES, E, SL * D)),
    }
    nc = bacc.Bacc("TRN2", target_bir_lowering=False, num_devices=1)
    aps = [nc.dram_tensor(f"in_{n}", a.shape, F32, kind="ExternalInput").ap() for n, a in arrays.items()]
    o = nc.dram_tensor("out_0", (BATCH, PATCHES + TEXT, D), F32, kind="ExternalOutput").ap()
    program(nc, *aps, o)
    r = run_bass_kernel_spmd(nc, [{f"in_{n}": a for n, a in arrays.items()}], core_ids=[0])
    return r.results[0]["out_0"]
```

```python
from contextlib import ExitStack

import concourse.bass as bass
from concourse import mybir
from concourse.alu_op_type import AluOpType as ALU

F32 = mybir.dt.float32
BF16 = mybir.dt.bfloat16
U32 = mybir.dt.uint32
I32 = mybir.dt.int32
ACT = mybir.ActivationFunctionType
AX_X = mybir.AxisListType.X

P = 128
D = 128
BATCH, PATCHES, TEXT = 16, 16, 128
PD = 768
PC = PD // P
H, DH = 8, 16
HL, HG = 4, 2
PH, HALF, E, K = 8, 64, 128, 8
NK = PH * K
PATCH_TILES = BATCH * PATCHES // P
TILES = PATCH_TILES + BATCH
GROUP = 4
GROUPS = BATCH // GROUP
GATHERED = GROUP - 1
EPS = 1e-5
QSCALE = DH ** -0.5
PAIRS = [(a, b) for a in range(K) for b in range(K) if (a + 1) * (b + 1) <= K]
NC = len(PAIRS)
QUARTERS = 4
CH = NK // QUARTERS
RSQRT_SEED = 1597463007.0
NEWTON = 3
SL = 4
SLICES = E // SL
TP = SL // 2
WBUF = 8
HOTS_BUF = 7
GELU_BUF = 6


def program(nc, patches, txt, tok_w, tok_b, w_q, w_kv, w_out, wq_ffn, bq, keys, table,
            down_t, up_t, out):
    ctx = ExitStack()
    with ctx:
        def sb(name, shape, dt=F32):
            return ctx.enter_context(nc.sbuf_tensor(name, shape, dt))

        def ps(name, shape):
            return ctx.enter_context(nc.psum_tensor(name, shape, F32))

        def sem(name):
            return ctx.enter_context(nc.semaphore(name))

        ones = sb("ones", [P, P])
        wv = sb("wv", [P, D])
        wqk = sb("wqk", [P, 2, HG, HL, 32])
        wout = sb("wout", [P, D])
        bqf = sb("bqf", [P, PH])
        mt = sb("mt", [P, 2, PH * E])
        bias = sb("bias", [P, 2 * PH])
        bparts = sb("bparts", [P, 3, 2 * PH], BF16)
        own = sb("own", [3 * 2 * PH, 2 * PH])
        brows = sb("brows", [3 * 2 * PH, 2 * PH, E], BF16)
        ones_b = sb("ones_b", [3 * 2 * PH, P], BF16)
        ident_b = sb("ident_b", [P, P], BF16)
        ident = sb("ident", [P, P])
        tri = sb("tri", [P, P])
        blk = sb("blk", [P, P])
        number = sb("number", [P, P])
        h0 = sb("h0", [P, 2, D])
        stats = sb("stats", [P, 6])
        mv = sb("mv", [P, 2])
        hv = sb("hv", [P, 1])
        bits = sb("bits", [P, 1], I32)
        y = sb("y", [P, 1])
        yt = sb("yt", [P, 1])
        xn = sb("xn", [P, D])
        xnT = sb("xnT", [P, P])
        qkT = sb("qkT", [P, 2 * HG, P])
        keep = sb("keep", [P, BATCH, 3, PATCHES])
        cur = sb("cur", [P, HG + H, PATCHES])
        cur_k = sb("cur_k", [P, HG, H * PATCHES])
        va = sb("va", [P, H, DH + 1])
        vpa = sb("vpa", [P, H, DH + 1])
        own_l = sb("own_l", [P, HL])
        own_h = sb("own_h", [P, H])
        pT = sb("pT", [P, H, P])
        hit = sb("hit", [P, NK, NC])
        pTp = hit[:].rearrange("p a b -> p (a b)")[:, 0:P]
        rden = sb("rden", [P, H])
        on = xn[:].rearrange("p (h j) -> p h j", j=DH)
        q2 = sb("q2", [P, D])
        q2T = sb("q2T", [P, P])
        onT = q2T
        top = sb("top", [P, 2, 2, PH, K])
        top_i = sb("top_i", [P, 2, PH, K], U32)
        cand = sb("cand", [P, 2, PH, NC])
        best = sb("best", [P, PH, K])
        best_p = sb("best_p", [P, PH, K], U32)
        best_f = sb("best_f", [P, NK])
        dif = sb("dif", [P, PH, K])
        ex = dif
        sm = sb("sm", [P, PH])
        idx = sb("idx", [P, GATHERED, NK], U32)
        wts = sb("wts", [P, GATHERED, NK])
        h1 = sb("h1", [P, GATHERED, D])
        qin = sb("qin", [P, GATHERED, D])
        rows = sb("rows", [P, NK, 2 * D])
        x = sb("x", [P, NK])
        g = sb("g", [P, NK])
        vals = sb("vals", [P, NK])
        res = sb("res", [P, GATHERED, D])
        h1d = sb("h1d", [P, D])
        q2Td = sb("q2Td", [P, P])
        lots = hit[:].rearrange("p a b -> p (a b)")[:, 0:6 * NK].rearrange("p (a h k) -> p a h k", a=3, h=2)
        ij = hit[:].rearrange("p a b -> p (a b)")[:, 6 * NK:8 * NK].bitcast(I32).rearrange("p (a k) -> p a k", a=2)
        wtd = sb("wtd", [P, NK])
        scal = sb("scal", [P, 4, NK])
        stage = sb("stage", [P, HOTS_BUF, 4 * TP * E])
        hot_ij = stage[:, :, 0:2 * TP * E].rearrange("p b (a n e) -> p b a n e", a=2, n=TP)
        hot_w = stage[:, :, 2 * TP * E:4 * TP * E].rearrange("p b (n h e) -> p b n h e", n=TP, h=2)
        halves = stage[:].rearrange("p b (c m) -> p (b c) m", c=2)
        act_x = halves[:, 0:GELU_BUF, :]
        wbuf = halves[:, GELU_BUF:GELU_BUF + WBUF, :]
        gd = sb("gd", [P, E * P])
        gd_j = gd[:].rearrange("p (j n) -> p j n", n=P)
        gd_h = gd[:].rearrange("p (j h n) -> p j h n", h=2, n=P // 2)
        resd = sb("resd", [P, D])
        at = [0]

        def early(*shape):
            n = 1
            for v in shape:
                n *= v
            view = gd[:, at[0]:at[0] + n]
            at[0] += n
            return view.rearrange("p (a b) -> p a b", b=shape[-1])

        wqk_in = early(1, 2 * D)
        btok = early(1, D)[0:1, 0, :]
        wtok, xpat = early(PC, D), early(PC, BATCH * PATCHES)
        wqf, keysT = early(PH, D), early(PH, E)

        A = ps("A", [P, 4, 512])
        B = ps("B", [P, 512])
        ACC = ps("ACC", [P, 4, D])
        X = ps("X", [P, 2, 512])

        s_tok, s_attn_w, s_ffn_w = sem("s_tok"), sem("s_attn_w"), sem("s_ffn_w")
        s_txt = [sem("s_txt0"), sem("s_txt1")]
        s_pool, s_const, s_wqk, s_ones = sem("s_pool"), sem("s_const"), sem("s_wqk"), sem("s_ones")
        s_fold, s_fold_c = sem("s_fold"), sem("s_fold_c")
        s_bias_split, s_bias = sem("s_bias_split"), sem("s_bias")
        s_emb_read, s_cur_k, s_vpa = sem("s_emb_read"), sem("s_cur_k"), sem("s_vpa")
        s_emb, s_xn, s_xnT_p, s_xnT = sem("s_emb"), sem("s_xn"), sem("s_xnT_p"), sem("s_xnT")
        s_qk_p, s_qk, s_v_p, s_v = sem("s_qk_p"), sem("s_qk"), sem("s_v_p"), sem("s_v")
        s_cur, s_s_p, s_sq, s_p = sem("s_cur"), sem("s_s_p"), sem("s_sq"), sem("s_p")
        s_o_p, s_on, s_onT_p, s_onT, s_y_p = sem("s_o_p"), sem("s_on"), sem("s_onT_p"), sem("s_onT"), sem("s_y_p")
        s_h1, s_q2, s_q2T_p, s_q2T, s_sc_p = sem("s_h1"), sem("s_q2"), sem("s_q2T_p"), sem("s_q2T"), sem("s_sc_p")
        s_topk, s_dif, s_ex = sem("s_topk"), sem("s_dif"), sem("s_ex")
        s_idx, s_res = sem("s_idx"), sem("s_res")
        s_rows = [sem(f"s_rows{c}") for c in range(PH)]
        s_x, s_g, s_vals, s_scaled, s_summed = sem("s_x"), sem("s_g"), sem("s_vals"), sem("s_scaled"), sem("s_summed")
        s_out = [sem(f"s_out{j}") for j in range(GATHERED)]
        s_lots, s_lots_p, s_scal = sem("s_lots"), sem("s_lots_p"), sem("s_scal")
        s_skip, s_resd, s_outd = sem("s_skip"), sem("s_resd"), sem("s_outd")
        s_hot, s_wgt_p, s_wgt = sem("s_hot"), sem("s_wgt_p"), sem("s_wgt")
        s_prod_p, s_gelu, s_weighed = sem("s_prod_p"), sem("s_gelu"), sem("s_weighed")
        s_table = [sem(f"s_table{n}") for n in range(WBUF)]
        s_sum_p = sem("s_sum_p")
        s_gathering, s_searching = sem("s_gathering"), sem("s_searching")
        s_dve = sem("s_dve")

        block = ctx.enter_context(nc.Block())

        def tile(i, j):
            return i * GATHERED + (2 + j)

        def quarters(i, j):
            if j == 0:
                return [(tile(i - 1, 1), 1, 2), (tile(i - 1, 1), 1, 3), (tile(i - 1, 2), 2, 0)]
            if j == 1:
                return [(tile(i - 1, 2), 2, q) for q in (1, 2, 3)]
            return [(tile(i, 0), 0, q) for q in (0, 1, 2)]

        def quarters_dense(i, first):
            own_quarters = [(tile(i - 1, 1), 1, 0), (tile(i - 1, 1), 1, 1)]
            return [None if first else (tile(i - 1, 0), 0, 3)] + own_quarters

        LAST = [(tile(GROUPS - 1, 0), 0, 3)] + [(tile(GROUPS - 1, j), j, q) for j in (1, 2) for q in range(QUARTERS)]

        @block.sync
        def _(sp):
            def load_txt(b, par):
                sp.dma_start(h0[:, par, :],
                             txt[bass.ds(b, 1), :, :].rearrange("o n d -> (o n) d")).then_inc(s_txt[par], 16)

            def store_patch(g, j):
                for m in range(P // PATCHES):
                    sp.dma_start(out[g * (P // PATCHES) + m, 0:PATCHES, :],
                                 res[m * PATCHES:(m + 1) * PATCHES, j, :]).then_inc(s_out[j], 16)

            def store_txt(b, src, done):
                sp.dma_start(out[bass.ds(b, 1), PATCHES:PATCHES + TEXT, :].rearrange("o n d -> (o n) d"),
                             src).then_inc(done, 16)

            def stream_down(i, slices):
                for s in slices:
                    if s >= WBUF:
                        sp.wait_ge(s_prod_p, i * SLICES + (s - WBUF + 1))
                    elif s == 0:
                        sp.wait_ge(s_wgt_p, i * SLICES + SLICES)
                    sp.dma_start(wbuf[:, s % WBUF, :], down_t[s, :, :]).then_inc(s_table[s % WBUF], 16)

            def stream_up(i, slices):
                for s in slices:
                    if s >= WBUF:
                        sp.wait_ge(s_sum_p, i * SLICES + (s - WBUF + 1))
                    else:
                        sp.wait_ge(s_prod_p, (i + 1) * SLICES - (WBUF - s - 1))
                    sp.dma_start(wbuf[:, s % WBUF, :], up_t[s, :, :]).then_inc(s_table[s % WBUF], 16)

            def dense(i, first=False):
                if not first:
                    stream_up(i - 1, range(WBUF, SLICES))
                f = i * GROUP + 2
                sp.wait_ge(s_h1, f + 1)
                load_txt(f, 0)
                if not first:
                    sp.wait_ge(s_res, tile(i - 1, 0) + 1)
                    store_txt(i * GROUP - 3, res[:, 0, :], s_out[0])

            def gathered(i, j, first=False, last=False):
                if j == 2:
                    stream_down(i, range(WBUF, SLICES))
                if not last or j == 0:
                    f = i * GROUP + (3 + j)
                    sp.wait_ge(s_h1, f + 1)
                    load_txt(f, (3 + j) % 2)
                if j == 0 and not first:
                    sp.wait_ge(s_resd, i)
                    store_txt(i * GROUP - GROUP, resd[:], s_outd)
                if j < 2:
                    sp.wait_ge(s_res, tile(i - 1, 1 + j) + 1)
                    if first:
                        store_patch(j, 1 + j)
                    else:
                        store_txt(i * GROUP - 2 + j, res[:, 1 + j, :], s_out[1 + j])
                if j == 1:
                    stream_down(i, range(WBUF))
                if j == 2:
                    stream_up(i, range(WBUF))

            sp.dma_start(xpat, patches).then_inc(s_tok, 16)
            sp.dma_start(wtok, tok_w).then_inc(s_tok, 16)
            sp.dma_start(btok, tok_b).then_inc(s_tok, 16)
            sp.dma_start(bqf[:], bq).then_inc(s_ffn_w, 16)
            sp.dma_start(wqf, wq_ffn).then_inc(s_ffn_w, 16)
            sp.dma_start(keysT, keys).then_inc(s_ffn_w, 16)
            for f in range(2):
                sp.wait_ge(s_h1, f + 1)
                load_txt(f, f)
            dense(0, first=True)
            for j in range(GATHERED):
                gathered(0, j, first=True)
            dense(1)
            with sp.Fori(1, GROUPS - 1) as i:
                for j in range(GATHERED):
                    gathered(i, j)
                dense(i + 1)
            for j in range(GATHERED):
                gathered(GROUPS - 1, j, last=True)
            stream_up(GROUPS - 1, range(WBUF, SLICES))
            sp.wait_ge(s_resd, GROUPS)
            store_txt(BATCH - GROUP, resd[:], s_outd)
            for j in range(GATHERED):
                sp.wait_ge(s_res, tile(GROUPS - 1, j) + 1)
                store_txt(BATCH - GATHERED + j, res[:, j, :], s_out[j])
            sp.wait_ge(s_outd, 16 * GROUPS)
            sp.wait_ge(s_out[0], 16 * GROUPS)
            for j in (1, 2):
                sp.wait_ge(s_out[j], 16 * (GROUPS + P // PATCHES))

        @block.gpsimd
        def _(pool):
            pool_count = [0]

            def link(ins):
                pool_count[0] += 1
                ins.then_inc(s_pool, 1)
                pool.wait_ge(s_pool, pool_count[0])

            link(nc.gpsimd.memset(ident[:], 0.0))
            link(nc.gpsimd.affine_select(out=ident[:], in_=ident[:], compare_op=ALU.not_equal, fill=1.0, base=0,
                                         pattern=[[-1, P]], channel_multiplier=1))
            link(nc.gpsimd.memset(tri[:], 1.0))
            link(nc.gpsimd.affine_select(out=tri[:], in_=tri[:], compare_op=ALU.is_ge, fill=0.0, base=0,
                                         pattern=[[1, P]], channel_multiplier=-1))
            blocks = blk[:].rearrange("p (b j) -> p b j", j=PATCHES)
            tris = tri[:].rearrange("p (b j) -> p b j", j=PATCHES)
            link(nc.gpsimd.affine_select(out=blocks, in_=tris, compare_op=ALU.is_ge, fill=0.0, base=0,
                                         pattern=[[-PATCHES, P // PATCHES], [0, PATCHES]], channel_multiplier=1))
            link(nc.gpsimd.affine_select(out=blocks, in_=blocks, compare_op=ALU.is_ge, fill=0.0, base=PATCHES - 1,
                                         pattern=[[PATCHES, P // PATCHES], [0, PATCHES]], channel_multiplier=-1))
            for mask, width in ((own_l, 32), (own_h, PATCHES)):
                n = P // width
                link(nc.gpsimd.memset(mask[:], 1.0))
                link(nc.gpsimd.affine_select(out=mask[:], in_=mask[:], compare_op=ALU.is_ge, fill=0.0, base=0,
                                             pattern=[[-width, n]], channel_multiplier=1))
                link(nc.gpsimd.affine_select(out=mask[:], in_=mask[:], compare_op=ALU.is_ge, fill=0.0, base=width - 1,
                                             pattern=[[width, n]], channel_multiplier=-1))
            link(nc.gpsimd.memset(own[:], 0.0))
            for r in range(3):
                link(nc.gpsimd.affine_select(out=own[:], in_=own[:], compare_op=ALU.not_equal, fill=1.0,
                                             base=-2 * PH * r, pattern=[[-1, 2 * PH]], channel_multiplier=1))
            nc.gpsimd.iota(number[:], pattern=[[1, P]], base=0, channel_multiplier=0,
                           allow_small_or_imprecise_dtypes=True).then_inc(s_const, 1)

            def gather(t, j, first=False):
                pool.wait_ge(s_idx, t + 1)
                for c in range(PH):
                    if c % 2 == 0 and not first:
                        pool.wait_ge(s_summed, (t - 1) * QUARTERS + (c // 2 + 1))
                        pool.sem_inc(s_gathering, 1)
                    for k in range(c * K, (c + 1) * K):
                        nc.gpsimd.indirect_dma_start(
                            rows[:, k, :], None, table,
                            bass.IndirectOffsetOnAxis(ap=idx[:, j, k:k + 1], axis=0)).then_inc(s_rows[c], 16)

            gather(0, 1, first=True)
            gather(1, 2)
            with pool.Fori(0, GROUPS) as i:
                for j in range(GATHERED):
                    gather(tile(i, j), j)

        PRODUCTS = [4, 4, 5, 1, 8, 3, 2, 5]
        WEIGHED = [2, 5, 6, 0, 5, 4, 4, 6]
        SUM = [5, 4, 5, 0, 7, 0, 2, 9]
        WEIGHTS = [[1, 2, 3, 0, 2, 1, 1, 6], [4, 2, 4, 0, 4, 0, 0, 2]]
        HOTS = [[3, 3, 2, 0, 4, 2, 0, 4], [3, 3, 4, 0, 4, 0, 0, 0]]

        def nothing(place):
            pass

        def spread(kind, i, counts, start=0, **how):
            def at(place):
                first = start + sum(counts[:place])
                kind(i, range(first, first + counts[place]), **how)
            return at

        @block.scalar
        def _(act):
            act.dma_start(wqk_in[:, 0, 0:D], w_q).then_inc(s_attn_w, 16)
            act.dma_start(wqk_in[:, 0, D:2 * D], w_kv[:, 0:D]).then_inc(s_attn_w, 16)
            act.dma_start(wv[:], w_kv[:, D:2 * D]).then_inc(s_attn_w, 16)
            act.dma_start(wout[:], w_out).then_inc(s_attn_w, 16)

            def gelu(t, q):
                act.wait_ge(s_x, t * QUARTERS + (q + 1))
                nc.scalar.activation(g[:, q * CH:(q + 1) * CH], x[:, q * CH:(q + 1) * CH],
                                     ACT.Gelu_apprx_tanh).then_inc(s_g, 1)

            def scale_up(t, q, first=0, last=CH):
                act.wait_ge(s_vals, t * QUARTERS + (q + 1))
                for k in range(q * CH + first, q * CH + last):
                    up = rows[:, k, D:2 * D]
                    ins = nc.scalar.activation(up, up, ACT.Copy, scale=vals[:, k:k + 1])
                    if k % 4 == 3:
                        ins.then_inc(s_scaled, 1)

            def copy_weights(i, slices):
                for s in slices:
                    act.wait_ge(s_wgt_p, i * SLICES + (s + 1))
                    nc.scalar.copy(gd_h[:, :, :, TP * s:TP * s + TP],
                                   X[:, s % 2, :].rearrange("p (n h j) -> p j h n", n=TP, h=2)).then_inc(s_wgt, 1)

            def gelu_dense(i, slices):
                for s in slices:
                    act.wait_ge(s_prod_p, i * SLICES + (s + 1))
                    if s >= GELU_BUF:
                        act.wait_ge(s_weighed, i * SLICES + (s - GELU_BUF + 1))
                    nc.scalar.activation(act_x[:, s % GELU_BUF, :], X[:, s % 2, :],
                                         ACT.Gelu_apprx_tanh).then_inc(s_gelu, 1)

            def project(f, patch=None, b=None, fill=nothing):
                act.wait_ge(s_xnT_p, f + 1)
                nc.scalar.copy(xnT[:], B[:, 0:P]).then_inc(s_xnT, 1)
                if patch is None:
                    image = keep[:, bass.ds(b, 1), :, :].rearrange("p o a j -> p (o a) j")
                    nc.scalar.copy(cur[:, 0:HG, :], image[:, 0:HG, :])
                    nc.scalar.copy(cur[:, HG:HG + H, :],
                                   image[:, HG:HG + 1, :].to_broadcast([P, H, PATCHES])).then_inc(s_cur, 1)
                fill(5)
                act.wait_ge(s_qk_p, f + 1)
                nc.scalar.copy(qkT[:].rearrange("p g n -> p (g n)"), B[:]).then_inc(s_qk, 1)
                if patch is not None:
                    act.wait_ge(s_qk, f + 1)
                    act.wait_ge(s_xnT, f + 1)
                    mine = keep[:, patch * 8:(patch + 1) * 8, :, :]
                    for n in range(HG):
                        nc.scalar.copy(mine[:, :, n, :], qkT[:, HG + n, :].rearrange("p (b j) -> p b j", j=PATCHES))
                    nc.scalar.copy(mine[:, :, 2, :],
                                   xnT[:].rearrange("p (b j) -> p b j", j=PATCHES)).then_inc(s_cur, 1)
                fill(6)
                act.wait_ge(s_v_p, f + 1)
                nc.scalar.copy(va[:, :, 0:DH], B[:, 0:P].rearrange("p (h j) -> p h j", j=DH)).then_inc(s_v, 1)

            def step(f, three, patch=None, dense=None, work=nothing, ahead=None):
                if three[0]:
                    gelu(three[0][0], three[0][2])
                act.wait_ge(s_s_p, f + 1)
                ins = nc.scalar.activation(pT[:].rearrange("p (l g) n -> p l (g n)", g=HG), A[:, :, 0:HG * P],
                                           ACT.Square, bias=1.0, scale=QSCALE)
                if patch is None:
                    ins = nc.scalar.activation(pTp, A[:, 0, HG * P:(HG + 1) * P], ACT.Square, bias=1.0, scale=QSCALE)
                ins.then_inc(s_sq, 1)
                work(0)
                if three[0]:
                    scale_up(three[0][0], three[0][2])
                work(1)
                act.wait_ge(s_onT_p, f + 1)
                nc.scalar.copy(onT[:], B[:, 0:P]).then_inc(s_onT, 1)
                if three[1]:
                    gelu(three[1][0], three[1][2])
                work(2)
                act.wait_ge(s_q2T_p, f + 1)
                nc.scalar.copy((q2T if dense is None else q2Td)[:], B[:, 2 * P:3 * P]).then_inc(s_q2T, 1)
                work(3)
                if three[1]:
                    scale_up(three[1][0], three[1][2])
                if three[2]:
                    gelu(three[2][0], three[2][2])
                work(4)
                if ahead:
                    project(*ahead, fill=work)
                else:
                    work(5)
                    work(6)
                if dense is None and three[2]:
                    scale_up(three[2][0], three[2][2])
                    work(7)
                act.wait_ge(s_dif, f + 1)
                nc.scalar.activation(ex[:], dif[:], ACT.Exp).then_inc(s_ex, 1)
                if dense is not None and three[2]:
                    scale_up(three[2][0], three[2][2])
                if dense is not None:
                    act.wait_ge(s_lots_p, dense + 1)
                    for n in range(2):
                        r = slice(n * NK, (n + 1) * NK)
                        lots_t = B[r, 0:3 * P].rearrange("p (a n) -> p a n", a=3)[:, :, r]
                        nc.scalar.copy(scal[r, 0:2, :], lots_t[:, 0:2, :])
                        ins = nc.scalar.copy(scal[r, 2 + n, :], lots_t[:, 2, :])
                    ins.then_inc(s_scal, 1)

            def dense_step(i, first=False):
                step(i * GROUP + 2, quarters_dense(i, first), dense=i,
                     ahead=(i * GROUP + 3, None, i * GROUP + 1))

            def gathered_step(i, j, last=False):
                work = [spread(copy_weights, i, WEIGHTS[0]), spread(copy_weights, i, WEIGHTS[1], sum(WEIGHTS[0])),
                        spread(gelu_dense, i, PRODUCTS)][j]
                step(i * GROUP + (3 + j), quarters(i, j), work=work,
                     ahead=None if last else (i * GROUP + (4 + j), None, i * GROUP + (2 + j)))

            act.wait_ge(s_fold, 1)
            nc.scalar.copy(mt[:].rearrange("p c n -> p (c n)"), A[:].rearrange("p a n -> p (a n)")).then_inc(s_fold_c, 1)
            project(0, patch=0)
            step(0, [None] * 3, patch=0, ahead=(1, 1))
            step(1, [None] * 3, patch=1, ahead=(2, None, 0))
            dense_step(0, first=True)
            for j in range(GATHERED):
                gathered_step(0, j)
            dense_step(1)
            with act.Fori(1, GROUPS - 1) as i:
                for j in range(GATHERED):
                    gathered_step(i, j)
                dense_step(i + 1)
            for j in range(GATHERED):
                gathered_step(GROUPS - 1, j, last=j == GATHERED - 1)
            for t, j, q in LAST:
                gelu(t, q)
                scale_up(t, q)

        @block.vector
        def _(dve):
            count = [0]

            def link(ins):
                count[0] += 1
                ins.then_inc(s_dve, 1)
                dve.wait_ge(s_dve, count[0])

            def clear():
                dve.sem_clear(s_dve)
                count[0] = 0

            def layernorm(dst, src, done):
                link(nc.vector.bn_stats(stats[:], src))
                link(nc.vector.bn_aggr(mv[:], stats[:]))
                link(nc.vector.tensor_scalar(yt[:], mv[:, 1:2], EPS, None, ALU.add))
                link(nc.vector.tensor_scalar(bits[:], yt[:].bitcast(I32), 1, None, ALU.logical_shift_right))
                nc.vector.tensor_scalar(y[:].bitcast(I32), bits[:], -1.0, RSQRT_SEED, ALU.mult, ALU.add)
                link(nc.vector.tensor_scalar(hv[:], yt[:], -0.5, None, ALU.mult))
                for _ in range(NEWTON):
                    link(nc.vector.scalar_tensor_tensor(yt[:], y[:], hv[:], y[:], ALU.mult, ALU.mult))
                    link(nc.vector.scalar_tensor_tensor(y[:], yt[:], 1.5, y[:], ALU.add, ALU.mult))
                nc.vector.tensor_scalar(dst, src, mv[:, 0:1], y[:], ALU.subtract, ALU.mult).then_inc(done, 1)

            def dots(t, j, q):
                for k in range(q * CH, (q + 1) * CH):
                    if k % K == 0:
                        dve.wait_ge(s_rows[k // K], t * (16 * K) + 16 * K)
                    last = nc.vector.tensor_tensor_reduce(rows[:, k, 0:D], rows[:, k, 0:D], qin[:, j, :], 1.0, 0.0,
                                                          ALU.mult, ALU.add, x[:, k:k + 1])
                last.then_inc(s_x, 1)

            def factors(t, j, q):
                part = slice(q * CH, (q + 1) * CH)
                dve.wait_ge(s_g, t * QUARTERS + (q + 1))
                nc.vector.tensor_tensor(vals[:, part], g[:, part], wts[:, j, part], ALU.mult).then_inc(s_vals, 1)

            def result(i, j, stored=True):
                dve.wait_ge(s_summed, tile(i, j) * QUARTERS + QUARTERS)
                if stored:
                    dve.wait_ge(s_out[j], i * 16 + (0 if j == 0 else 16 * (P // PATCHES)))
                nc.vector.tensor_reduce(res[:, j, :], ACC[:].rearrange("p a d -> p d a"), AX_X,
                                        ALU.add).then_inc(s_res, 1)

            def search(f, write, between, middle, later):
                for a in range(4):
                    dve.wait_ge(s_sc_p, f * 4 + (a + 1))
                    dve.sem_inc(s_searching, 1)
                    for n in range(4 * a, 4 * a + 4):
                        last = nc.vector.max(top[:, 0, n // PH, n % PH, :], A[:, a, (n % 4) * E:(n % 4 + 1) * E])
                link(last)
                for n in range(2 * PH):
                    last = nc.vector.max_index(top_i[:, n // PH, n % PH, :], top[:, 0, n // PH, n % PH, :],
                                               A[:, n // 4, (n % 4) * E:(n % 4 + 1) * E])
                last.then_inc(s_topk, 1)
                between()
                dve.wait_ge(s_topk, f + 1)
                nc.vector.tensor_scalar(top[:, 1, 0, :, :], top_i[:, 0, :, :], float(E), None, ALU.mult)
                link(nc.vector.tensor_copy(top[:, 1, 1, :, :], top_i[:, 1, :, :]))
                at = 0
                for a, nb in [(a, K // (a + 1)) for a in range(4)]:
                    nc.vector.tensor_tensor(
                        cand[:, :, :, at:at + nb],
                        top[:, :, 0, :, a:a + 1].to_broadcast([P, 2, PH, nb]), top[:, :, 1, :, 0:nb], ALU.add)
                    at += nb
                link(nc.vector.tensor_tensor(cand[:, :, :, at:NC], top[:, :, 0, :, 4:K],
                                             top[:, :, 1, :, 0:1].to_broadcast([P, 2, PH, K - 4]), ALU.add))
                for h in range(PH):
                    last = nc.vector.max(best[:, h, :], cand[:, 0, h, :])
                link(last)
                middle()
                for h in range(PH):
                    last = nc.vector.max_index(best_p[:, h, :], best[:, h, :], cand[:, 0, h, :])
                link(last)
                link(nc.vector.tensor_copy(best_f[:], best_p[:].rearrange("p h k -> p (h k)")))
                link(nc.vector.tensor_tensor(hit[:], best_f[:].unsqueeze(2).to_broadcast([P, NK, NC]),
                                             number[:, 0:NC].unsqueeze(1).to_broadcast([P, NK, NC]), ALU.is_equal))
                hits = hit[:].rearrange("p (h k) n -> p h k n", k=K)
                link(nc.vector.tensor_tensor(hits, hits, cand[:, 1, :, :].unsqueeze(2).to_broadcast([P, PH, K, NC]),
                                             ALU.mult))
                link(nc.vector.tensor_reduce(best_f[:], hit[:], AX_X, ALU.add))
                later()
                write()
                nc.vector.tensor_tensor(dif[:], best[:], best[:, :, 0:1].to_broadcast([P, PH, K]),
                                        ALU.subtract).then_inc(s_dif, 1)

            def softmax(f, dst):
                dve.wait_ge(s_ex, f + 1)
                link(nc.vector.tensor_reduce(sm[:], ex[:], AX_X, ALU.add))
                link(nc.vector.reciprocal(sm[:], sm[:]))
                link(nc.vector.tensor_tensor(dst.rearrange("p (h k) -> p h k", k=K), ex[:],
                                             sm[:].unsqueeze(2).to_broadcast([P, PH, K]), ALU.mult))

            def one_hots(i, slices, first=False):
                for s in slices:
                    if s == 0:
                        dve.wait_ge(s_scal, i + 1)
                    if s >= HOTS_BUF or not first:
                        dve.wait_ge(s_wgt_p, i * SLICES + (s - HOTS_BUF + 1))
                    buf, cols = s % HOTS_BUF, slice(TP * s, TP * s + TP)
                    link(nc.vector.tensor_tensor(
                        hot_ij[:, buf, :, :, :], number[:].unsqueeze(1).unsqueeze(1).to_broadcast([P, 2, TP, E]),
                        scal[:, 0:2, cols].unsqueeze(3).to_broadcast([P, 2, TP, E]), ALU.is_equal))
                    nc.vector.tensor_tensor(
                        hot_w[:, buf, :, :, :], hot_ij[:, buf, 1, :, :].unsqueeze(2).to_broadcast([P, TP, 2, E]),
                        scal[:, 2:4, cols].rearrange("p h n -> p n h").unsqueeze(3).to_broadcast([P, TP, 2, E]),
                        ALU.mult).then_inc(s_hot, 1)

            def weigh(i, slices):
                for s in slices:
                    dve.wait_ge(s_gelu, i * SLICES + (s + 1))
                    part = gd[:, s * SL * P:(s + 1) * SL * P]
                    nc.vector.tensor_tensor(part, part, act_x[:, s % GELU_BUF, :], ALU.mult).then_inc(s_weighed, 1)

            def normalize(f, par, patch=None):
                if patch is None:
                    dve.wait_ge(s_txt[par], (f - par) * 8)
                layernorm(xn[:], h0[:, par, :], s_xn)

            def patch_keys(f):
                dve.wait_ge(s_cur, f + 1)
                for n in range(HG):
                    own_cols = cur_k[:, n, n * HL * PATCHES:(n + 1) * HL * PATCHES].rearrange("p (l j) -> p l j", l=HL)
                    last = nc.vector.tensor_tensor(own_cols, cur[:, n:n + 1, :].to_broadcast([P, HL, PATCHES]),
                                                   own_l[:].unsqueeze(2).to_broadcast([P, HL, PATCHES]), ALU.mult)
                last.then_inc(s_cur_k, 1)
                dve.wait_ge(s_v, f + 1)
                nc.vector.tensor_tensor(vpa[:, :, 0:DH], B[:, P:2 * P].rearrange("p (h j) -> p h j", j=DH),
                                        own_h[:].unsqueeze(2).to_broadcast([P, H, DH]), ALU.mult).then_inc(s_vpa, 1)

            def step(f, par, j, three, patch=None, dense=None, hots=nothing, weighs=nothing, ahead=None,
                     before=None, at_start=None, before_search=None, at_end=None):
                src = h0[:, par, :]
                if three[0]:
                    dots(*three[0])
                if before is not None:
                    softmax(f - 1, wts[:, before, :])
                hots(0)
                if at_start:
                    at_start()
                dve.wait_ge(s_sq, f + 1)
                mask = (tri if patch is None else blk)[:].unsqueeze(1).to_broadcast([P, H, P])
                nc.vector.scalar_tensor_tensor(pT[:], pT[:], 1.0, mask, ALU.add, ALU.mult).then_inc(s_p, 1)
                if three[0]:
                    factors(*three[0])
                weighs(0)
                if patch == 0:
                    dve.wait_ge(s_fold, 2)
                    nc.vector.tensor_copy(bias[:, 0:PH], X[:, 0, 0:PH])
                    link(nc.vector.tensor_copy(bias[:, PH:2 * PH], X[:, 1, 0:PH]))
                    for r in range(2):
                        link(nc.vector.tensor_copy(bparts[:, r, :], bias[:]))
                        link(nc.vector.tensor_tensor(bias[:], bias[:], bparts[:, r, :], ALU.subtract))
                    nc.vector.tensor_copy(bparts[:, 2, :], bias[:]).then_inc(s_bias_split, 1)
                if three[1]:
                    dots(*three[1])
                dve.wait_ge(s_o_p, f + 1)
                o = B[:, 2 * P:2 * P + H * (DH + 1)].rearrange("p (h j) -> p h j", j=DH + 1)
                link(nc.vector.tensor_scalar(rden[:].unsqueeze(2), o[:, :, DH:DH + 1], 2 * EPS, None, ALU.max))
                link(nc.vector.reciprocal(rden[:], rden[:]))
                nc.vector.tensor_tensor(on, o[:, :, 0:DH], rden[:].unsqueeze(2).to_broadcast([P, H, DH]),
                                        ALU.mult).then_inc(s_on, 1)
                if patch == 0:
                    dve.wait_ge(s_fold, 3)
                    nc.vector.tensor_tensor(
                        brows[:], X[0:3 * 2 * PH, 0:1, 0:E].to_broadcast([3 * 2 * PH, 2 * PH, E]),
                        own[:].unsqueeze(2).to_broadcast([3 * 2 * PH, 2 * PH, E]), ALU.mult).then_inc(s_bias, 1)
                hots(1)
                weighs(1)
                if three[1]:
                    factors(*three[1])
                resid = h1d[:] if dense is not None else h1[:, j, :]
                if dense is not None and three[0]:
                    dve.wait_ge(s_skip, dense)
                dve.wait_ge(s_y_p, f + 1)
                nc.vector.tensor_tensor(resid, src, B[:, P:2 * P], ALU.add).then_inc(s_h1, 1)
                dve.wait_ge(s_h1, f + 1)
                layernorm(q2[:] if dense is not None else qin[:, j, :], resid, s_q2)
                hots(2)
                weighs(2)
                if before_search:
                    before_search()
                if ahead:
                    normalize(*ahead)
                if three[2]:
                    dots(*three[2])

                def between():
                    hots(4)
                    weighs(4)
                    if three[2]:
                        factors(*three[2])

                def middle():
                    hots(5)
                    weighs(5)

                def later():
                    hots(6)
                    weighs(6)

                if dense is None:
                    search(f, lambda: nc.vector.tensor_copy(idx[:, j, :], best_f[:]).then_inc(s_idx, 1),
                           between, middle, later)
                else:
                    def split():
                        link(nc.vector.tensor_copy(best_p[:].rearrange("p h k -> p (h k)"), best_f[:]))
                        number_i = best_p[:].rearrange("p h k -> p (h k)").bitcast(I32)
                        nc.vector.tensor_scalar(ij[:, 0, :], number_i, E.bit_length() - 1, None, ALU.logical_shift_right)
                        link(nc.vector.tensor_scalar(ij[:, 1, :], number_i, E - 1, None, ALU.bitwise_and))
                        nc.vector.tensor_copy(lots[:, 0:2, :, :], ij[:].unsqueeze(2).to_broadcast([P, 2, 2, NK]))

                    search(f, split, between, middle, later)
                    softmax(f, wtd[:])
                    nc.vector.tensor_copy(lots[:, 2, :, :],
                                          wtd[:].unsqueeze(1).to_broadcast([P, 2, NK])).then_inc(s_lots, 1)
                if ahead and ahead[2] is None:
                    patch_keys(ahead[0])
                hots(7)
                weighs(7)
                if at_end:
                    at_end()
                clear()

            def result_dense(i):
                dve.wait_ge(s_sum_p, i * SLICES + SLICES)
                nc.vector.tensor_copy(resd[:], X[:, 0, 0:D]).then_inc(s_resd, 1)

            def dense_step(i, first=False, second=False):
                step(i * GROUP + 2, 0, None, quarters_dense(i, first), dense=i,
                     ahead=(i * GROUP + 3, 1, None), before=GATHERED - 1,
                     before_search=None if first else lambda: result(i - 1, 0, not second),
                     at_start=None if first or second else lambda: dve.wait_ge(s_outd, (i - 1) * 16))

            def gathered_step(i, j, first=False, last=False):
                step(i * GROUP + (3 + j), (3 + j) % 2, j, quarters(i, j),
                     before=j - 1 if j else None,
                     hots=[spread(one_hots, i, HOTS[0], first=first),
                           spread(one_hots, i, HOTS[1], sum(HOTS[0]), first=first), nothing][j],
                     weighs=spread(weigh, i, WEIGHED) if j == 2 else nothing,
                     ahead=None if last else (i * GROUP + (4 + j), (4 + j) % 2, None),
                     at_start=[None if first else lambda: result_dense(i - 1), None,
                               lambda: result(i - 1, 2, not first)][j],
                     at_end=(lambda: result(i - 1, 1, not first)) if j == 0 else None)

            nc.vector.memset(ones[:], 1.0)
            nc.vector.memset(ones_b[:], 1.0).then_inc(s_ones, 1)
            nc.vector.memset(va[:], 1.0)
            nc.vector.memset(cur_k[:], 0.0)
            nc.vector.memset(scal[:], 0.0)
            link(nc.vector.memset(wqk[:], 0.0))
            dve.wait_ge(s_attn_w, 64)
            nc.vector.tensor_copy(wqk[:].rearrange("p a g l j -> p (a g l) j")[:, :, 0:DH],
                                  wqk_in.rearrange("p o (a j) -> p (o a) j", j=DH)).then_inc(s_wqk, 1)
            dve.wait_ge(s_const, 1)
            nc.vector.tensor_copy(vpa[:, :, DH:DH + 1], own_h[:].unsqueeze(2))
            nc.vector.tensor_copy(ident_b[:], ident[:]).then_inc(s_ones, 1)
            dve.wait_ge(s_emb, 1)
            link(nc.vector.tensor_copy(h0[:, 0, :], B[:, 3 * P:4 * P]))
            normalize(0, 0, 0)
            dve.wait_ge(s_emb, 2)
            nc.vector.tensor_copy(h0[:, 1, :], ACC[:, 0, :]).then_inc(s_emb_read, 1)
            dve.wait_ge(s_emb_read, 1)
            step(0, 0, 1, [None] * 3, patch=0, ahead=(1, 1, 1))
            step(1, 1, 2, [None] * 3, patch=1, ahead=(2, 0, None), before=1)
            dense_step(0, first=True)
            for j in range(GATHERED):
                gathered_step(0, j, first=True)
            dense_step(1, second=True)
            with dve.Fori(1, GROUPS - 1) as i:
                for j in range(GATHERED):
                    gathered_step(i, j)
                dense_step(i + 1)
            for j in range(GATHERED):
                gathered_step(GROUPS - 1, j, last=j == GATHERED - 1)
            softmax(TILES - 1, wts[:, GATHERED - 1, :])
            i = GROUPS - 1
            for n in range(len(LAST)):
                dots(*LAST[n])
                factors(*LAST[n])
                if n == 0:
                    result(i, 0)
                if n == 7:
                    dve.wait_ge(s_outd, i * 16)
                    result_dense(i)
                if n == 4:
                    result(i, 1)
            result(i, 2)

        @block.tensor
        def _(pe):
            mm = nc.tensor.matmul

            def fold_keys():
                pe.wait_ge(s_ffn_w, 48)
                for c in range(2):
                    r = slice(c * HALF, (c + 1) * HALF)
                    for h in range(PH):
                        last = mm(A[:, 2 * c + h // 4, (h % 4) * E:(h % 4 + 1) * E], wqf[r, h, :], keysT[r, h, :],
                                  start=True, stop=True)
                last.then_inc(s_fold, 1)

            def fold_bias():
                for c in range(2):
                    r = slice(c * HALF, (c + 1) * HALF)
                    for h in range(PH):
                        last = mm(X[:, c, h:h + 1], keysT[r, h, :], bqf[r, h:h + 1], start=True, stop=True)
                last.then_inc(s_fold, 1)

            def turn_bias():
                pe.wait_ge(s_bias_split, 1)
                pe.wait_ge(s_ones, 2)
                mm(X[0:3 * 2 * PH, 0, 0:E], bparts[:].rearrange("p r n -> p (r n)"), ident_b[:], start=True,
                   stop=True).then_inc(s_fold, 1)

            def sum_up(t, j, q, first=False):
                group = CH // 4
                if q == 0 and not first:
                    pe.wait_ge(s_res, t)
                for n in range(q * group, (q + 1) * group):
                    pe.wait_ge(s_scaled, t * (NK // 4) + (n + 1))
                    last = mm(ACC[:], ident[:], rows[:, 4 * n:4 * n + 4, D:2 * D], start=n == 0,
                              stop=n == NK // 4 - 1)
                    if n == 0:
                        mm(ACC[:, 0, :], ident[:], h1[:, j, :], start=False, stop=False)
                last.then_inc(s_summed, 1)

            def table(i, s, base):
                pe.wait_ge(s_table[s % WBUF], i * (2 * SLICES // WBUF * 16) + (base // WBUF + s // WBUF + 1) * 16)
                return wbuf[:, s % WBUF, :].rearrange("p (j n) -> p j n", n=P)

            def weights(i, slices, first=False):
                for s in slices:
                    pe.wait_ge(s_hot, i * SLICES + (s + 1))
                    if s >= 2:
                        pe.wait_ge(s_wgt, i * SLICES + (s - 1))
                    elif not first:
                        pe.wait_ge(s_resd, i)
                    for n in range(TP):
                        last = mm(X[:, s % 2, n * 2 * P:(n + 1) * 2 * P], hot_ij[:, s % HOTS_BUF, 0, n, :],
                                  hot_w[:, s % HOTS_BUF, n, :, :].rearrange("p h e -> p (h e)"), start=True, stop=True)
                    last.then_inc(s_wgt_p, 1)

            def products(i, slices):
                for s in slices:
                    w = table(i, s, 0)
                    if s >= 2:
                        pe.wait_ge(s_gelu, i * SLICES + (s - 1))
                    else:
                        pe.wait_ge(s_wgt, i * SLICES + (SLICES - 1 + s))
                    for n in range(SL):
                        last = mm(X[:, s % 2, n * P:(n + 1) * P], w[:, n, :], q2Td[:], start=True, stop=True)
                    last.then_inc(s_prod_p, 1)

            def sums(i, slices):
                for s in slices:
                    w = table(i, s, SLICES)
                    if s == 0:
                        pe.wait_ge(s_weighed, i * SLICES + SLICES)
                        mm(X[:, 0, 0:D], ident[:], h1d[:], start=True, stop=False).then_inc(s_skip, 1)
                    for n in range(SL):
                        last = mm(X[:, 0, 0:D], gd_j[:, s * SL + n, :], w[:, n, :], start=False,
                                  stop=s * SL + n == E - 1)
                    last.then_inc(s_sum_p, 1)

            def project(f, patch=None, fill=nothing):
                if patch == 0:
                    for g, to in ((0, B[:, 3 * P:4 * P]), (1, ACC[:, 0, :])):
                        for c in range(PC):
                            mm(to, xpat[:, c, g * P:(g + 1) * P], wtok[:, c, :], start=c == 0, stop=False)
                        mm(to, ones[0:1, :], btok, start=False, stop=True).then_inc(s_emb, 1)
                    fold_keys()
                pe.wait_ge(s_xn, f + 1)
                nc.tensor.transpose(B[:, 0:P], xn[:], ident[:]).then_inc(s_xnT_p, 1)
                fill(5)
                pe.wait_ge(s_xnT, f + 1)
                for n in range(2 * HG):
                    last = mm(B[:, n * P:(n + 1) * P], wqk[:, n // HG, n % HG, :, :].rearrange("p l j -> p (l j)"),
                              xnT[:], start=True, stop=True)
                last.then_inc(s_qk_p, 1)
                fill(6)
                if patch == 0:
                    pe.wait_ge(s_fold_c, 1)
                pe.wait_ge(s_qk, f + 1)
                last = mm(B[:, 0:P], xnT[:], wv[:], start=True, stop=True)
                if patch is None:
                    pe.wait_ge(s_cur, f + 1)
                    last = mm(B[:, P:2 * P], cur[:, HG:HG + H, :].rearrange("p h j -> p (h j)"), wv[:],
                              start=True, stop=True)
                last.then_inc(s_v_p, 1)

            def step(f, j, three, work, patch=None, dense=None, ahead=None, before_output=None):
                if patch != 0:
                    pe.wait_ge(s_topk, f)
                for h in range(H):
                    l, n = h % HL, h // HL
                    r = slice(32 * l, 32 * l + DH)
                    last = mm(A[:, l, n * P:(n + 1) * P], qkT[r, HG + n, :], qkT[r, n, :], start=True, stop=True)
                if patch is None:
                    pe.wait_ge(s_cur_k, f - 1)
                    for n in range(HG):
                        last = mm(A[:, 0, HG * P:(HG + 1) * P], cur_k[:, n, :], qkT[:, n, :],
                                  start=n == 0, stop=n == HG - 1)
                last.then_inc(s_s_p, 1)
                if patch == 0:
                    fold_bias()
                work(0)
                pe.wait_ge(s_v, f + 1)
                pe.wait_ge(s_p, f + 1)
                if before_output:
                    before_output()
                if patch is None:
                    pe.wait_ge(s_vpa, f - 1)
                    to = B[:, 2 * P:2 * P + H * (DH + 1)]
                    mm(to, ones[:], vpa[:].rearrange("p h j -> p (h j)"), start=True, stop=False)
                    mm(to, pTp, vpa[:].rearrange("p h j -> p (h j)"), start=False, stop=False)
                for h in range(H):
                    l, n = h % HL, h // HL
                    last = mm(B[:, 2 * P + h * (DH + 1):2 * P + (h + 1) * (DH + 1)], pT[:, l * HG + n, :], va[:, h, :],
                              start=patch is not None, stop=patch is not None or h == H - 1)
                last.then_inc(s_o_p, 1)
                if patch == 0:
                    turn_bias()
                work(1)
                pe.wait_ge(s_on, f + 1)
                nc.tensor.transpose(B[:, 0:P], xn[:], ident[:]).then_inc(s_onT_p, 1)
                pe.wait_ge(s_onT, f + 1)
                mm(B[:, P:2 * P], onT[:], wout[:], start=True, stop=True).then_inc(s_y_p, 1)
                if three[0]:
                    sum_up(*three[0])
                work(2)
                pe.wait_ge(s_q2, f + 1)
                nc.tensor.transpose(B[:, 2 * P:3 * P], q2[:] if dense is not None else qin[:, j, :],
                                    ident[:]).then_inc(s_q2T_p, 1)
                work(3)
                pe.wait_ge(s_q2T, f + 1)
                if patch == 0:
                    pe.wait_ge(s_bias, 1)
                inputs = q2T if dense is None else q2Td
                for a in range(4):
                    mm(A[:, a, :], inputs[:], mt[:, a // 2, (a % 2) * 512:(a % 2 + 1) * 512], start=True, stop=False)
                    mm(A[:, a, :], ones_b[:], brows[:, 4 * a:4 * a + 4, :].rearrange("p n e -> p (n e)"), start=False,
                       stop=True).then_inc(s_sc_p, 1)
                if three[1]:
                    sum_up(*three[1])
                work(4)
                if ahead:
                    project(*ahead, fill=work)
                else:
                    work(5)
                    work(6)
                work(7)
                if three[2]:
                    sum_up(*three[2])
                if dense is not None:
                    pe.wait_ge(s_vpa, f)
                    pe.wait_ge(s_lots, dense + 1)
                    for n in range(3):
                        last = nc.tensor.transpose(B[:, n * P:(n + 1) * P], lots[:, n, :, :].rearrange("p a n -> p (a n)"),
                                                   ident[:])
                    last.then_inc(s_lots_p, 1)

            def dense_step(i, first=False):
                three = quarters_dense(i, first)
                if first:
                    three[1] = (*three[1], True)
                step(i * GROUP + 2, None, three, nothing if first else spread(sums, i - 1, SUM), dense=i,
                     ahead=(i * GROUP + 3,))

            def gathered_step(i, j, first=False, last=False):
                work = [spread(weights, i, WEIGHTS[0], first=first), spread(weights, i, WEIGHTS[1], sum(WEIGHTS[0])),
                        spread(products, i, PRODUCTS)][j]
                step(i * GROUP + (3 + j), j, quarters(i, j), work, ahead=None if last else (i * GROUP + (4 + j),),
                     before_output=(lambda: pe.wait_ge(s_scal, i + 1)) if j == 0 else None)

            pe.wait_ge(s_const, 1)
            pe.wait_ge(s_wqk, 1)
            pe.wait_ge(s_ones, 1)
            pe.wait_ge(s_tok, 48)
            project(0, 0)
            step(0, 1, [None] * 3, nothing, patch=0, ahead=(1, 1))
            step(1, 2, [None] * 3, nothing, patch=1, ahead=(2,))
            dense_step(0, first=True)
            for j in range(GATHERED):
                gathered_step(0, j, first=True)
            dense_step(1)
            with pe.Fori(1, GROUPS - 1) as i:
                for j in range(GATHERED):
                    gathered_step(i, j)
                dense_step(i + 1)
            for j in range(GATHERED):
                gathered_step(GROUPS - 1, j, last=j == GATHERED - 1)
            for n in range(len(LAST)):
                sums(GROUPS - 1, range(min(n * 4, SLICES), min((n + 1) * 4, SLICES)))
                sum_up(*LAST[n])


def kernel(x, txt, L0_tok_W, L0_tok_b, L0_attn_w_q, L0_attn_w_kv, L0_attn_w_out, L0_ffn_Wq, L0_ffn_bq,
           L0_ffn_keys, L0_ffn_w_down_embed, L0_ffn_w_up_embed):
    import numpy as np
    import concourse.bacc as bacc
    from concourse.bass_utils import run_bass_kernel_spmd

    con = np.ascontiguousarray
    side = 4
    pat = np.asarray(x).reshape(BATCH, 3, side, 16, side, 16).transpose(1, 3, 5, 0, 2, 4)
    pat = con(pat.reshape(PC, P, BATCH * PATCHES).transpose(1, 0, 2))
    arrays = {
        "patches": pat,
        "txt": con(txt),
        "tok_w": con(np.asarray(L0_tok_W).T.reshape(PC, P, D).transpose(1, 0, 2)),
        "tok_b": con(np.asarray(L0_tok_b).reshape(1, D)),
        "w_q": con(L0_attn_w_q),
        "w_kv": con(L0_attn_w_kv),
        "w_out": con(L0_attn_w_out),
        "wq_ffn": con(np.asarray(L0_ffn_Wq).reshape(PH, P, D).transpose(1, 0, 2)),
        "bq": con(np.asarray(L0_ffn_bq).reshape(PH, P).T),
        "keys": con(np.asarray(L0_ffn_keys).transpose(1, 3, 0, 2).reshape(P, PH, E)),
        "table": con(np.concatenate([L0_ffn_w_down_embed, L0_ffn_w_up_embed], axis=1)),
        "down_t": con(np.asarray(L0_ffn_w_down_embed).reshape(E, SLICES, SL, D).transpose(1, 3, 2, 0)
                      .reshape(SLICES, D, SL * E)),
        "up_t": con(np.asarray(L0_ffn_w_up_embed).reshape(E, SLICES, SL, D).transpose(1, 0, 2, 3)
                    .reshape(SLICES, E, SL * D)),
    }
    nc = bacc.Bacc("TRN2", target_bir_lowering=False, num_devices=1)
    aps = [nc.dram_tensor(f"in_{n}", a.shape, F32, kind="ExternalInput").ap() for n, a in arrays.items()]
    o = nc.dram_tensor("out_0", (BATCH, PATCHES + TEXT, D), F32, kind="ExternalOutput").ap()
    program(nc, *aps, o)
    r = run_bass_kernel_spmd(nc, [{f"in_{n}": a for n, a in arrays.items()}], core_ids=[0])
    return r.results[0]["out_0"]
```
